# Optimizing a Trainium2 kernel written in Bass

```python
import numpy as np
import jax
import jax.numpy as jnp

def _softmax(x, axis=-1):
    return jax.nn.softmax(x, axis=axis)

def _gelu(x):
    return jax.nn.gelu(x, approximate=True)

def _silu(x):
    return jax.nn.silu(x)

def _sigmoid(x):
    return jax.nn.sigmoid(x)

def _layernorm(x, axis=-1, eps=1e-05):
    m = jnp.mean(x, axis=axis, keepdims=True)
    v = jnp.var(x, axis=axis, keepdims=True)
    return (x - m) / jnp.sqrt(v + eps)

def _scatter_add(tgt, idx, src, axis=0):
    return tgt.at[idx].add(src)

def _segment_sum(src, seg, n):
    return jax.ops.segment_sum(src, seg, n)
kernel_name = 'mk_seq_preln_d1_jaxref_r8_d16aee'

def setup_inputs(seed: int=0):
    np.random.seed(seed)
    _w = jnp.asarray

    def _L0_attn_setup():
        import jax, jax.numpy as jnp
        import numpy as np
        LN_EPS = 1e-05

        def _phi(x):
            return jax.nn.elu(x) + 1.0
        key = jax.random.key(seed)
        ks = jax.random.split(key, 5)
        B, N, D = (4, 1024, 128)
        s = 1.0 / np.sqrt(D)
        return {'H': jax.random.normal(ks[0], (B, N, D), dtype=jnp.float32), 'W_qkv': jax.random.normal(ks[1], (3 * D, D), dtype=jnp.float32) * s, 'b_qkv': jax.random.normal(ks[2], (3 * D,), dtype=jnp.float32) * 0.01, 'W_proj': jax.random.normal(ks[3], (D, D), dtype=jnp.float32) * s, 'b_proj': jax.random.normal(ks[4], (D,), dtype=jnp.float32) * 0.01, 'gamma': jnp.ones((D,), dtype=jnp.float32), 'beta': jnp.zeros((D,), dtype=jnp.float32)}
    _L0_attn_in = _L0_attn_setup()

    def _L0_ffn_setup():
        import jax, jax.numpy as jnp
        import numpy as np
        D_MODEL = 128
        HIDDEN = 512
        N_EXPERTS = 8
        TOP_K = 2
        key = jax.random.key(seed)
        k_x, k_r, k_w1, k_w2 = jax.random.split(key, 4)
        x = jax.random.normal(k_x, (2, 128, D_MODEL), dtype=jnp.float32)
        Wr = jax.random.normal(k_r, (D_MODEL, N_EXPERTS), dtype=jnp.float32) * 0.02
        W1 = jax.random.normal(k_w1, (N_EXPERTS, D_MODEL, HIDDEN), dtype=jnp.float32) * 0.02
        W2 = jax.random.normal(k_w2, (N_EXPERTS, HIDDEN, D_MODEL), dtype=jnp.float32) * 0.02
        return {'x': x, 'Wr': Wr, 'W1': W1, 'W2': W2}
    _L0_ffn_in = _L0_ffn_setup()
    _d = {'L0_attn_H': _L0_attn_in['H'], 'L0_attn_W_qkv': _L0_attn_in['W_qkv'], 'L0_attn_b_qkv': _L0_attn_in['b_qkv'], 'L0_attn_W_proj': _L0_attn_in['W_proj'], 'L0_attn_b_proj': _L0_attn_in['b_proj'], 'L0_attn_gamma': _L0_attn_in['gamma'], 'L0_attn_beta': _L0_attn_in['beta'], 'L0_ffn_Wr': _L0_ffn_in['Wr'], 'L0_ffn_W1': _L0_ffn_in['W1'], 'L0_ffn_W2': _L0_ffn_in['W2']}
    _x0 = _d['L0_attn_H']
    _d['L0_attn_H'] = jax.random.normal(jax.random.fold_in(jax.random.key(seed), 1), (16, 256, 128), dtype=_x0.dtype)
    del _x0
    return _d

def reference(L0_attn_H, L0_attn_W_qkv, L0_attn_b_qkv, L0_attn_W_proj, L0_attn_b_proj, L0_attn_gamma, L0_attn_beta, L0_ffn_Wr, L0_ffn_W1, L0_ffn_W2):

    def _L0_attn_ref(H, W_qkv, b_qkv, W_proj, b_proj, gamma, beta):
        import jax, jax.numpy as jnp
        import numpy as np
        LN_EPS = 1e-05

        def _phi(x):
            return jax.nn.elu(x) + 1.0
        B, N, D = H.shape
        num_heads = 16
        head_dim = D // num_heads
        residual = H
        qkv = jnp.einsum('bnd,ed->bne', H, W_qkv) + b_qkv
        qkv = qkv.reshape(B, N, 3, num_heads, head_dim).transpose(2, 0, 3, 1, 4)
        q, k, v = (qkv[0], qkv[1], qkv[2])
        q = _phi(q)
        k = _phi(k)
        kv = jnp.einsum('bhnd,bhnv->bhdv', k, v)
        k1 = k.sum(axis=2)
        qkv_out = jnp.einsum('bhnd,bhdv->bhnv', q, kv)
        qk1 = jnp.sum(q * k1[:, :, None, :], axis=-1, keepdims=True)
        out = qkv_out / jnp.clip(qk1, 1e-06, None)
        out = out.reshape(B, N, D)
        out = jnp.einsum('bnd,ed->bne', out, W_proj) + b_proj
        mu = out.mean(axis=-1, keepdims=True)
        var = out.var(axis=-1, keepdims=True)
        out = (out - mu) * jax.lax.rsqrt(var + LN_EPS) * gamma + beta
        return out + residual

    def _L0_ffn_ref(x, Wr, W1, W2):
        import jax, jax.numpy as jnp
        import numpy as np
        D_MODEL = 128
        HIDDEN = 512
        N_EXPERTS = 8
        TOP_K = 2
        B, S, D = x.shape
        flat = x.reshape(-1, D)
        logits = flat @ Wr
        top_vals, top_idx = jax.lax.top_k(logits, TOP_K)
        weights = jax.nn.softmax(top_vals, axis=-1)
        top1 = top_idx[:, 0]
        w_top1 = weights[:, 0]
        h = jax.nn.gelu(jnp.einsum('td,edh->teh', flat, W1), approximate=False)
        y = jnp.einsum('teh,ehd->ted', h, W2)
        y_sel = jnp.take_along_axis(y, top1[:, None, None], axis=1)[:, 0, :]
        out = (w_top1[:, None] * y_sel).reshape(B, S, D)
        return out
    x = L0_attn_H
    x = x + _L0_attn_ref(_layernorm(x, axis=-1), L0_attn_W_qkv, L0_attn_b_qkv, L0_attn_W_proj, L0_attn_b_proj, L0_attn_gamma, L0_attn_beta)
    x = x + _L0_ffn_ref(_layernorm(x, axis=-1), L0_ffn_Wr, L0_ffn_W1, L0_ffn_W2)
    return x

_drawn_inputs = setup_inputs


def setup_inputs(seed=0):
    import zlib

    import numpy as np

    out = dict(_drawn_inputs(seed))
    spreads = {'L0_attn_gamma': (1.0, 0.2), 'L0_attn_beta': (0.0, 0.1)}
    factors = {'L0_ffn_Wr': 4.756, 'L0_ffn_W1': 4.547, 'L0_ffn_W2': 4.492}
    for name, (base, spread) in spreads.items():
        noise = np.random.default_rng([zlib.crc32(name.encode()), seed]).standard_normal(out[name].shape)
        drawn = base * np.exp(spread * noise) if base else spread * noise
        out[name] = jnp.asarray(drawn.astype(out[name].dtype))
    for name, factor in factors.items():
        out[name] = (out[name] * factor).astype(out[name].dtype)
    return out
```

```python
from contextlib import ExitStack

import concourse.bass as bass
from concourse import mybir

ALU = mybir.AluOpType
ACT = mybir.ActivationFunctionType
AX = mybir.AxisListType
F32 = mybir.dt.float32
F16 = mybir.dt.float16
BF16 = mybir.dt.bfloat16
I32 = mybir.dt.int32

P = 128
LN_EPS = 1e-5
DEN_MIN = 1e-6
NEG_HUGE = -3.0e38


class Item:

    def __init__(self, unroll, j, c, j_min=0):
        self.unroll, self.j, self.c = unroll, j, c
        self.n = unroll * j + c
        self.least = unroll * (j if isinstance(j, int) else j_min) + c

    def slot(self, k):
        return self.c % k

    def round(self):
        return self.j + self.c // self.unroll

    def least_round(self):
        return self.least // self.unroll


def build(nc, x, wqkv_t, b_all, wproj_t, gamma, beta, w_router, w1, w2, out):
    D = wproj_t.shape[0]
    TOK = x.shape[0] * x.shape[1] * x.shape[2] // D
    E = w_router.shape[1]
    HID = w1.shape[1] // E
    HEADS = 16
    HD = D // HEADS
    CH = HID // P
    TB = 2
    SEQ = TB * P
    NB = TOK // SEQ
    VW = D + HEADS
    UB = 4
    PT = 2 * TB
    REGION = TOK + P
    ROW = D + 4
    MEAN, RSTD, GATE, TOKEN = D, D + 1, D + 2, D + 3
    NT = TOK // P + E - 1
    UT = 6
    LAG_B, LAG_T = 4, 5
    assert D == P and NB % UB == 0 and HID % P == 0

    R = SEQ // HEADS
    assert R == HEADS == 16
    rows_dram = nc.dram_tensor("expert_rows", [E * REGION, ROW], F32, kind="Internal").ap()

    with ExitStack() as ctx:
        def sb(name, shape, dt=F32):
            return ctx.enter_context(nc.sbuf_tensor(name, shape, dt))

        def ps(name, shape):
            return ctx.enter_context(nc.psum_tensor(name, shape, F32))

        def sem(name):
            return ctx.enter_context(nc.semaphore(name))

        wqkv = sb("wqkv", [P, 3 * D])
        wproj = sb("wproj", [P, D])
        wr = sb("wr", [P, E])
        w1_sb = sb("w1_sb", [P, E * HID])
        w2_sb = sb("w2_sb", [P, E * HID])
        gamma_b = sb("gamma_b", [P, D])
        beta_b = sb("beta_b", [P, D])
        bias_f = sb("bias_f", [P, 4 * D])
        bias_r = sb("bias_r", [P, 4 * D])
        bias_s = sb("bias_s", [P, 4 * D])
        bias3 = sb("bias3", [P, 4 * D], BF16)
        bias_h = sb("bias_h", [P, 4 * D], BF16)
        bias_m = sb("bias_m", [P, 4 * D], BF16)
        ones_b = sb("ones_b", [P, SEQ], BF16)
        ones_h = sb("ones_h", [P, P], F16)
        before = sb("before", [P, P], F16)
        ident = sb("ident", [P, P])
        head_mask = sb("head_mask", [P, VW])
        neg_half = sb("neg_half", [P, TB])
        first_key = sb("first_key", [P, PT, E])
        token_no = sb("token_no", [P, NB * TB], I32)
        region_base = sb("region_base", [P, E])
        step_128 = sb("step_128", [P, E, TOK // P])
        upto = sb("upto", [P, E, E])
        tile_no = sb("tile_no", [P, NT])
        tile_end = sb("tile_end", [P, NT])
        pad_rows = sb("pad_rows", [P, ROW])

        x_sb = sb("x_sb", [P, NB, SEQ])
        stat1 = sb("stat1", [P, 2, TB, 6])
        mv1 = sb("mv1", [P, 2, TB, 2])
        var1 = sb("var1", [P, 2, TB])
        rstd1 = sb("rstd1", [P, 2, TB])
        nb1 = sb("nb1", [P, 2, TB])
        rp1 = sb("rp1", [P, 2, TB])
        xn = sb("xn", [P, 2, TB, D])
        xx = sb("xx", [P, 2, TB, D])
        resid = sb("resid", [P, UB, TB, D])
        xnT = sb("xnT", [P, 2, SEQ])
        exp_q = sb("exp_q", [P, 2, SEQ])
        exp_k = sb("exp_k", [P, 2, TB, D])
        phi_q = sb("phi_q", [P, 2, SEQ])
        phi_k = sb("phi_k", [P, 2, TB, D])
        v_sb = sb("v_sb", [P, 2, TB, VW])
        kv_sb = sb("kv_sb", [P, 2, VW])
        den = sb("den", [P, 2, TB, HEADS])
        rden = sb("rden", [P, 2, TB, HEADS])
        attn = sb("attn", [P, 2, HD, 2 * HEADS])
        regrouped = sb("regrouped", [P, 2, TB, HD, R])
        attnT = sb("attnT", [P, 2, SEQ])
        stat2 = sb("stat2", [P, 2, TB, 6])
        mv2 = sb("mv2", [P, 2, TB, 2])
        var2 = sb("var2", [P, 2, TB])
        rstd2 = sb("rstd2", [P, 2, TB])
        scaled = sb("scaled", [P, 2, TB, D])
        rows = sb("rows", [P, UB, TB, ROW])
        stat3 = sb("stat3", [P, 2, TB, 6])
        var3 = sb("var3", [P, 2, TB])
        mv3 = sb("mv3", [P, 2, TB, 2])
        nb3 = sb("nb3", [P, 2, TB])
        xn3 = sb("xn3", [P, 2, TB, D])
        xn3T = sb("xn3T", [P, 2, SEQ])
        top1 = sb("top1", [P, PT])
        is_top = sb("is_top", [P, PT, E])
        key = sb("key", [P, PT, E])
        top_key = sb("top_key", [P, PT])
        chosen = sb("chosen", [P, PT, E], F16)
        rest = sb("rest", [P, PT, E])
        top2 = sb("top2", [P, PT])
        gap = sb("gap", [P, PT])
        exp_gap = sb("exp_gap", [P, PT])
        gate_den = sb("gate_den", [P, PT])
        n_chosen = sb("n_chosen", [P, E])
        seen = sb("seen", [P, E], F16)
        pos_sel = sb("pos_sel", [P, PT, E])
        pos = sb("pos", [P, 2, PT], I32)
        n_tok = sb("n_tok", [P, E])
        over = sb("over", [P, E, TOK // P])
        n_tiles = sb("n_tiles", [P, E])
        tiles_m = sb("tiles_m", [P, E, E])
        tiles_upto = sb("tiles_upto", [P, E])
        tiles_before = sb("tiles_before", [P, E])
        row_base = sb("row_base", [P, E])
        reached = sb("reached", [P, NT, E + 1])
        mine = sb("mine", [P, NT, E])
        row_of = sb("row_of", [P, NT, E])
        row_sel = sb("row_sel", [P, NT, E])
        passed = sb("passed", [P, NT])
        tile_row = sb("tile_row", [P, NT], I32)
        tile_expert = sb("tile_expert", [P, NT], I32)

        got = sb("got", [P, UT, ROW])
        got_n = sb("got_n", [P, 2, D])
        got_T = sb("got_T", [P, 2, P])
        w1_tile = sb("w1_tile", [P, 2, HID])
        hid = sb("hid", [P, 2, CH, P])
        done = sb("done", [P, UT, D])
        done_token = sb("done_token", [P, UT], I32)

        bank = [ps(f"bank{i}", [P, 512]) for i in range(8)]
        xnT_ps = bank[0][:, 0:SEQ]
        attnT_ps = bank[1][:, 0:SEQ]
        xn3T_ps = bank[2][:, 0:SEQ]
        q_ps = bank[3][:, 0:SEQ]
        kv_ps = bank[4][:, :].rearrange("p (t c) -> p t c", t=TB)
        num_ps = bank[5][:, 0:TB * VW].rearrange("p (t c) -> p t c", t=TB)
        sum_ps = bank[5][:, TB * VW:TB * VW + VW]
        proj_ps = bank[6][:, 0:SEQ].rearrange("p (t c) -> p t c", t=TB)
        logit_ps = bank[7][:, 0:PT * E].rearrange("p (t e) -> p t e", t=PT)
        rank_ps = bank[7][:, 64:64 + PT * E].rearrange("p (t e) -> p t e", t=PT)
        count_ps = bank[7][:, 128:128 + E]
        got_ps = [bank[0 + h][:, 0:P] for h in range(2)]
        hid_ps = [bank[2 + h][:, :].rearrange("p (c t) -> p c t", c=CH) for h in range(2)]
        y_ps = [bank[4 + h][:, 0:D] for h in range(2)]

        S = {n: sem(n) for n in (
            "weights_in", "bias_in", "affine_in", "ffn_in", "pads_in",
            "pool_const", "dve_const", "bias_step", "mask_step",
            "stats1_done", "mv1_done", "var1_done", "rstd1_done", "nb1_done", "xn_done", "xx_done",
            "resid_done", "xnT_in_ps", "xnT_done", "q_in_ps", "kv_in_ps", "expk_done", "v_done",
            "expq_done", "phik_done", "phiq_done", "sum_in_ps", "kvsum_done", "num_in_ps",
            "den_done", "rden_done", "attn_done", "regrouped_done", "attnT_in_ps", "attnT_done", "proj_in_ps",
            "stats2_done", "mv2_done", "var2_done", "rstd2_done", "scaled_done", "x1_done",
            "stats3_done", "mv3_done", "var3_done", "rstd3_done", "nb3_done", "xn3_done",
            "xn3T_in_ps", "xn3T_done", "logits_in_ps", "top1_done", "is_top_done", "key_done",
            "top_key_done", "chosen_done", "rest_done", "top2_done", "gap_done", "exp_gap_done",
            "gate_den_done", "n_chosen_done", "ranks_in_ps", "pos_sel_done", "seen_done", "pos_done",
            "token_done", "counts_in_ps", "table_step", "table_done",
            "got_n_done", "got_in_ps", "got_T_done", "w1_tile_done", "hid_in_ps", "hid_done",
            "y_in_ps", "done_ready", "passed_gate")}
        x_in = [sem(f"x_in{c}") for c in range(4)]
        rows_free = [sem(f"rows_free{h}") for h in range(2)]
        got_in = [sem(f"got_in{h}") for h in range(UT)]
        out_done = [sem(f"out_done{h}") for h in range(UT)]

        X_CHUNKS = [(0, 1), (1, 2), (2, 4), (4, NB)]

        def pass_1(eng, step):
            def peeled(s):
                def at(lag):
                    return Item(UB, (s - lag) // UB, (s - lag) % UB) if 0 <= s - lag < NB else None
                step(s % UB, at)
            first = 2 * UB
            for s in range(first):
                peeled(s)
            with eng.Fori(first // UB, NB // UB) as j:
                for u in range(UB):
                    step(u, lambda lag: Item(UB, j, u - lag, first // UB))
            for s in range(NB, NB + LAG_B + 1):
                peeled(s)

        def pass_2(eng, step):
            def peeled(s):
                def at(lag):
                    return Item(UT, (s - lag) // UT, (s - lag) % UT) if 0 <= s - lag < NT else None
                step(at)
            first = 2 * UT
            for s in range(first):
                peeled(s)
            with eng.Fori(first // UT, NT // UT) as j:
                for u in range(UT):
                    step(lambda lag: Item(UT, j, u - lag, first // UT))
            for s in range(NT // UT * UT, NT + LAG_T):
                peeled(s)

        def pair(b):
            return UB // 2 * b.j + b.c // 2

        def x_tile(b, t):
            return x_sb[:, bass.ds(b.n, 1), t * D:t * D + D].rearrange("p a d -> p (a d)")

        block = ctx.enter_context(nc.Block())

        @block.sync
        def _(sp):
            def load_x(c):
                lo, hi = X_CHUNKS[c]
                sp.dma_start(x_sb[:, lo:hi, :], x[:, lo:hi, :]).then_inc(x_in[c], 16)
            load_x(0)
            sp.dma_start(wqkv[:, :], wqkv_t).then_inc(S["weights_in"], 16)
            load_x(1)
            load_x(2)
            sp.dma_start(wproj[:, :], wproj_t).then_inc(S["weights_in"], 16)
            sp.dma_start(wr[:, :], w_router).then_inc(S["weights_in"], 16)
            load_x(3)
            sp.dma_start(w1_sb[:, :], w1).then_inc(S["ffn_in"], 16)
            sp.dma_start(w2_sb[:, :], w2).then_inc(S["ffn_in"], 16)
            sp.wait_ge(S["pool_const"], 1)
            sp.dma_start(rows_dram.rearrange("(e r) c -> r e c", e=E)[0:P],
                         pad_rows[:, :].unsqueeze(1).to_broadcast([P, E, ROW])).then_inc(S["pads_in"], 16)

            sp.wait_ge(S["table_done"], 1)
            sp.wait_ge(S["pads_in"], 16)
            for h in range(2):
                sp.wait_ge(rows_free[h], 16 * PT * (NB // UB))

            def step(at):
                t = at(0)
                if t is not None:
                    row = sp.value_load(tile_row[0:1, bass.ds(t.n, 1)], min_val=0, max_val=E * REGION - P)
                    if t.least >= UT:
                        sp.wait_ge(S["done_ready"], t.n - UT + 1)
                    sp.dma_start(got[:, t.slot(UT), :], rows_dram[bass.ds(row, P), :])\
                      .then_inc(got_in[t.slot(UT)], 16)
            pass_2(sp, step)
            for h in range(UT):
                sp.wait_ge(out_done[h], 16 * ((NT - 1 - h) // UT + 1))

        @block.gpsimd
        def _(pool):
            g = nc.gpsimd
            g.memset(pad_rows[:, :], 0.0).then_inc(S["mask_step"], 1)
            pool.wait_ge(S["mask_step"], 1)
            g.iota(pad_rows[:, TOKEN:TOKEN + 1].bitcast(I32), pattern=[[1, 1]], base=TOK,
                   channel_multiplier=1).then_inc(S["pool_const"], 1)
            g.memset(neg_half[:, :], -0.5)
            g.memset(ident[:, :], 0.0).then_inc(S["mask_step"], 1)
            pool.wait_ge(S["mask_step"], 2)
            g.affine_select(out=ident[:, :], in_=ident[:, :], compare_op=ALU.not_equal, fill=1.0,
                            base=0, pattern=[[-1, P]], channel_multiplier=1).then_inc(S["pool_const"], 1)
            g.memset(head_mask[:, :], 1.0).then_inc(S["mask_step"], 1)
            pool.wait_ge(S["mask_step"], 3)
            parts = [(head_mask[:, 0:D], [[-HD, HEADS], [0, HD]]), (head_mask[:, D:VW], [[-HD, HEADS]])]
            for m, pat in parts:
                g.affine_select(out=m, in_=m, compare_op=ALU.is_ge, fill=0.0, base=0, pattern=pat,
                                channel_multiplier=1).then_inc(S["mask_step"], 1)
            pool.wait_ge(S["mask_step"], 5)
            for m, pat in parts:
                g.affine_select(out=m, in_=m, compare_op=ALU.is_ge, fill=0.0, base=HD - 1,
                                pattern=[[-a, n] for a, n in pat], channel_multiplier=-1)\
                 .then_inc(S["pool_const"], 1)

            def more_constants():
                g.memset(before[:, :], 1.0).then_inc(S["mask_step"], 1)
                g.memset(upto[:, :, :], 1.0).then_inc(S["mask_step"], 1)
                pool.wait_ge(S["mask_step"], 7)
                g.affine_select(out=before[:, :], in_=before[:, :], compare_op=ALU.is_gt, fill=0.0, base=0,
                                pattern=[[1, P]], channel_multiplier=-1)
                g.affine_select(out=upto[:, :, :], in_=upto[:, :, :], compare_op=ALU.is_ge, fill=0.0,
                                base=0, pattern=[[1, E], [-1, E]], channel_multiplier=0)
                g.iota(first_key[:, :, :], pattern=[[0, PT], [-1, E]], base=E, channel_multiplier=0,
                       allow_small_or_imprecise_dtypes=True)
                g.iota(seen[:, :], pattern=[[REGION // P, E]], base=1, channel_multiplier=0,
                       allow_small_or_imprecise_dtypes=True)
                g.iota(token_no[:, :].rearrange("p (b t) -> p b t", t=TB), pattern=[[SEQ, NB], [1, TB]],
                       base=0, channel_multiplier=TB)
                g.iota(region_base[:, :], pattern=[[REGION, E]], base=P, channel_multiplier=0,
                       allow_small_or_imprecise_dtypes=True)
                g.iota(step_128[:, :, :], pattern=[[0, E], [P, TOK // P]], base=0, channel_multiplier=0,
                       allow_small_or_imprecise_dtypes=True)
                g.iota(tile_no[:, :], pattern=[[1, NT]], base=0, channel_multiplier=0,
                       allow_small_or_imprecise_dtypes=True)
                g.iota(tile_end[:, :], pattern=[[P, NT]], base=P, channel_multiplier=0,
                       allow_small_or_imprecise_dtypes=True).then_inc(S["pool_const"], 1)

            def scatter(p_slot, half, tiles):
                for t in tiles:
                    g.indirect_dma_start(
                        out=rows_dram, out_offset=bass.IndirectOffsetOnAxis(ap=pos[:, half, t:t + 1], axis=0),
                        in_=rows[:, 2 * half + t // TB, t % TB, :], in_offset=None,
                        bounds_check=E * REGION - 1, oob_is_err=False).then_inc(rows_free[half], 16)

            def step(u, at):
                b0, b3, b4, b5 = at(0), at(3), at(4), at(5)
                if b0 is not None:
                    h = b0.slot(2)
                    pool.wait_ge(S["var1_done"], b0.n + 1)
                    g.tensor_tensor(rstd1[:, h, :], var1[:, h, :], neg_half[:, :], ALU.pow)\
                     .then_inc(S["rstd1_done"], 1)
                if b0 is not None and b0.least == 0 and isinstance(b0.n, int):
                    more_constants()
                if b3 is not None:
                    h = b3.slot(2)
                    pool.wait_ge(S["var2_done"], b3.n + 1)
                    g.tensor_tensor(rstd2[:, h, :], var2[:, h, :], neg_half[:, :], ALU.pow)\
                     .then_inc(S["rstd2_done"], 1)
                if b5 is not None and b5.c % 2 == 1:
                    scatter(b5, (b5.c // 2) % 2, range(PT // 2, PT))
                if b0 is not None:
                    h = b0.slot(2)
                    pool.wait_ge(S["xx_done"], b0.n + 1)
                    g.tensor_tensor(resid[:, b0.slot(UB), :, :], xx[:, h, :, :],
                                    beta_b[:, :].unsqueeze(1).to_broadcast([P, TB, D]), ALU.add)\
                     .then_inc(S["resid_done"], 1)
                if b3 is not None:
                    h = b3.slot(2)
                    pool.wait_ge(S["var3_done"], b3.n + 1)
                    g.tensor_tensor(rows[:, b3.slot(UB), :, RSTD], var3[:, h, :], neg_half[:, :], ALU.pow)\
                     .then_inc(S["rstd3_done"], 1)
                    g.tensor_copy(rows[:, b3.slot(UB), :, TOKEN].bitcast(I32),
                                  token_no[:, bass.ds(TB * b3.n, TB)]).then_inc(S["token_done"], 1)
                if b4 is not None and b4.c % 2 == 1:
                    pool.wait_ge(S["pos_done"], pair(b4) + 1)
                    pool.wait_ge(S["token_done"], b4.n + 1)
                    pool.wait_ge(S["rstd3_done"], b4.n + 1)
                    pool.sem_inc(S["passed_gate"], 1)
                    scatter(b4, (b4.c // 2) % 2, range(PT // 2))
            pass_1(pool, step)

            def step(at):
                t = at(5)
                if t is not None:
                    pool.wait_ge(S["done_ready"], t.n + 1)
                    pool.sem_inc(S["passed_gate"], 1)
                    g.indirect_dma_start(
                        out=out, out_offset=bass.IndirectOffsetOnAxis(
                            ap=done_token[:, t.slot(UT):t.slot(UT) + 1], axis=0),
                        in_=done[:, t.slot(UT), :], in_offset=None, bounds_check=TOK - 1, oob_is_err=False).then_inc(out_done[t.slot(UT)], 16)
            pass_2(pool, step)

        @block.tensor
        def _(pe):
            t_ = nc.tensor
            pe.wait_ge(S["pool_const"], 4)
            pe.wait_ge(S["dve_const"], 2)

            def step(u, at):
                b1, b2, b3, b4 = at(1), at(2), at(3), at(4)
                if b3 is not None:
                    h = b3.slot(2)
                    pe.wait_ge(S["regrouped_done"], b3.n + 1)
                    for t in range(TB):
                        mm = t_.transpose(attnT_ps[:, P * t:P * t + P], regrouped[:, h, t, :, :].rearrange("p d r -> p (d r)"), ident[:, :])
                    mm.then_inc(S["attnT_in_ps"], 1)
                if b4 is not None:
                    h = b4.slot(2)
                    pe.wait_ge(S["xn3_done"], b4.n + 1)
                    for t in range(TB):
                        mm = t_.transpose(xn3T_ps[:, P * t:P * t + P], xn3[:, h, t, :], ident[:, :])
                    mm.then_inc(S["xn3T_in_ps"], 1)
                if b1 is not None:
                    h = b1.slot(2)
                    pe.wait_ge(S["xn_done"], b1.n + 1)
                    for t in range(TB):
                        mm = t_.transpose(xnT_ps[:, P * t:P * t + P], xn[:, h, t, :], ident[:, :])
                    mm.then_inc(S["xnT_in_ps"], 1)
                if b3 is not None:
                    h = b3.slot(2)
                    pe.wait_ge(S["attnT_done"], b3.n + 1)
                    for t in range(TB):
                        t_.matmul(proj_ps[:, t, :], ones_b[:, 0:P], bias3[:, 3 * D:4 * D], start=True, stop=False)
                        mm = t_.matmul(proj_ps[:, t, :], attnT[:, h, P * t:P * t + P], wproj[:, :],
                                       start=False, stop=True)
                    mm.then_inc(S["proj_in_ps"], 1)
                if b2 is not None:
                    h = b2.slot(2)
                    pe.wait_ge(S["phik_done"], b2.n + 1)
                    pe.wait_ge(S["v_done"], b2.n + 1)
                    for t in range(TB):
                        mm = t_.matmul(sum_ps, phi_k[:, h, t, :], v_sb[:, h, t, :],
                                       start=t == 0, stop=t == TB - 1)
                    mm.then_inc(S["sum_in_ps"], 1)
                if b4 is not None:
                    h = b4.slot(2)
                    pe.wait_ge(S["xn3T_done"], b4.n + 1)
                    if b4.c % 2 == 0 and b4.least >= 2:
                        pe.wait_ge(S["pos_done"], pair(b4))
                    for t in range(TB):
                        mm = t_.matmul(logit_ps[:, TB * h + t, :], xn3T[:, h, P * t:P * t + P], wr[:, :],
                                       start=True, stop=True)
                    mm.then_inc(S["logits_in_ps"], 1)
                if b1 is not None:
                    h = b1.slot(2)
                    pe.wait_ge(S["xnT_done"], b1.n + 1)
                    for t in range(TB):
                        t_.matmul(kv_ps[:, t, :], ones_b[:, 0:P], bias3[:, D:3 * D], start=True, stop=False)
                        mm = t_.matmul(kv_ps[:, t, :], xnT[:, h, P * t:P * t + P], wqkv[:, D:3 * D],
                                       start=False, stop=True)
                    mm.then_inc(S["kv_in_ps"], 1)
                    if b1.least >= 1:
                        pe.wait_ge(S["phiq_done"], b1.n)
                    t_.matmul(q_ps, bias3[:, 0:D], ones_b[:, :], start=True, stop=False)
                    t_.matmul(q_ps, wqkv[:, 0:D], xnT[:, h, :], start=False, stop=True)\
                      .then_inc(S["q_in_ps"], 1)
                if b2 is not None:
                    h = b2.slot(2)
                    pe.wait_ge(S["kvsum_done"], b2.n + 1)
                    pe.wait_ge(S["phiq_done"], b2.n + 1)
                    for t in range(TB):
                        mm = t_.matmul(num_ps[:, t, :], phi_q[:, h, P * t:P * t + P], kv_sb[:, h, :],
                                       start=True, stop=True)
                    mm.then_inc(S["num_in_ps"], 1)
                if b4 is not None and b4.c % 2 == 1:
                    n = pair(b4)
                    if b4.least == 1:
                        pe.wait_ge(S["pool_const"], 5)
                    pe.wait_ge(S["rest_done"], n + 1)
                    if b4.least >= 2:
                        pe.wait_ge(S["seen_done"], n)
                    t_.matmul(rank_ps, ones_h[:, :], seen[:, :].unsqueeze(1).to_broadcast([P, PT, E]),
                              start=True, stop=False)
                    for t in range(PT - 1):
                        t_.matmul(rank_ps[:, t + 1:PT, :], ones_h[:, :],
                                  chosen[:, t:t + 1, :].to_broadcast([P, PT - 1 - t, E]),
                                  start=False, stop=False)
                    t_.matmul(rank_ps, before[:, :], chosen[:, :, :], start=False, stop=True)\
                      .then_inc(S["ranks_in_ps"], 1)

            pe.wait_ge(S["weights_in"], 48)
            pass_1(pe, step)
            pe.wait_ge(S["seen_done"], NB // 2)
            t_.matmul(count_ps, ones_h[:, :], seen[:, :], start=True, stop=True).then_inc(S["counts_in_ps"], 1)

            pe.wait_ge(S["ffn_in"], 32)
            pe.wait_ge(S["table_done"], 1)

            def step(at):
                t3, t4, t5 = at(3), at(4), at(5)
                if t3 is not None:
                    h = t3.slot(2)
                    pe.wait_ge(S["got_n_done"], t3.n + 1)
                    t_.transpose(got_ps[h], got_n[:, h, :], ident[:, :]).then_inc(S["got_in_ps"], 1)
                if t4 is not None:
                    h = t4.slot(2)
                    pe.wait_ge(S["got_T_done"], t4.n + 1)
                    pe.wait_ge(S["w1_tile_done"], t4.n + 1)
                    for c in range(CH):
                        mm = t_.matmul(hid_ps[h][:, c, :], w1_tile[:, h, P * c:P * c + P], got_T[:, h, :],
                                       start=True, stop=True)
                    mm.then_inc(S["hid_in_ps"], 1)
                if t5 is not None:
                    h = t5.slot(2)
                    expert = pe.value_load(tile_expert[0:1, bass.ds(t5.n, 1)], min_val=0, max_val=E - 1)
                    pe.wait_ge(S["hid_done"], t5.n + 1)
                    if t5.least >= 2:
                        pe.wait_ge(S["done_ready"], t5.n - 1)
                    for c in range(CH):
                        mm = t_.matmul(y_ps[h], hid[:, h, c, :], w2_sb[:, bass.ds(expert * HID + P * c, P)],
                                       start=c == 0, stop=c == CH - 1)
                    mm.then_inc(S["y_in_ps"], 1)
            pass_2(pe, step)

        @block.scalar
        def _(act):
            a = nc.scalar
            for r in range(3):
                act.dma_start(bias_f[32 * r:32 * r + 1, :], b_all[r:r + 1, :]).then_inc(S["bias_in"], 16)
            act.dma_start(gamma_b[:, :], gamma.partition_broadcast(P)).then_inc(S["affine_in"], 16)
            act.dma_start(beta_b[:, :], beta.partition_broadcast(P)).then_inc(S["affine_in"], 16)

            def step(u, at):
                b0, b1, b3, b4 = at(0), at(1), at(3), at(4)
                if b3 is not None:
                    act.wait_ge(S["attnT_in_ps"], b3.n + 1)
                    a.copy(attnT[:, b3.slot(2), :], attnT_ps).then_inc(S["attnT_done"], 1)
                if b4 is not None:
                    act.wait_ge(S["xn3T_in_ps"], b4.n + 1)
                    a.copy(xn3T[:, b4.slot(2), :], xn3T_ps).then_inc(S["xn3T_done"], 1)
                if b1 is not None:
                    act.wait_ge(S["xnT_in_ps"], b1.n + 1)
                    a.copy(xnT[:, b1.slot(2), :], xnT_ps).then_inc(S["xnT_done"], 1)
                if b0 is not None:
                    h = b0.slot(2)
                    act.wait_ge(S["nb1_done"], b0.n + 1)
                    for t in range(TB):
                        i = a.activation(xn[:, h, t, :], x_tile(b0, t),
                                         ACT.Identity, bias=nb1[:, h, t:t + 1], scale=rstd1[:, h, t:t + 1])
                    i.then_inc(S["xn_done"], 1)
                    for t in range(TB):
                        i = a.activation(xx[:, h, t, :], x_tile(b0, t),
                                         ACT.Identity, bias=nb1[:, h, t:t + 1], scale=rp1[:, h, t:t + 1])
                    i.then_inc(S["xx_done"], 1)
                if b1 is not None:
                    h = b1.slot(2)
                    act.wait_ge(S["kv_in_ps"], b1.n + 1)
                    a.activation(exp_k[:, h, :, :], kv_ps[:, :, 0:D], ACT.Exp, bias=-1.0).then_inc(S["expk_done"], 1)
                    a.copy(v_sb[:, h, :, 0:D], kv_ps[:, :, D:2 * D]).then_inc(S["v_done"], 1)
                    act.wait_ge(S["q_in_ps"], b1.n + 1)
                    a.activation(exp_q[:, h, :], q_ps, ACT.Exp, bias=-1.0).then_inc(S["expq_done"], 1)
                if b4 is not None and b4.c % 2 == 1:
                    act.wait_ge(S["gap_done"], pair(b4) + 1)
                    a.activation(exp_gap[:, :], gap[:, :], ACT.Exp).then_inc(S["exp_gap_done"], 1)
                if b3 is not None:
                    h = b3.slot(2)
                    act.wait_ge(S["nb3_done"], b3.n + 1)
                    act.wait_ge(S["rstd3_done"], b3.n + 1)
                    for t in range(TB):
                        i = a.activation(xn3[:, h, t, :], rows[:, b3.slot(UB), t, 0:D], ACT.Identity,
                                         bias=nb3[:, h, t:t + 1], scale=rows[:, b3.slot(UB), t, RSTD:RSTD + 1])
                    i.then_inc(S["xn3_done"], 1)
            pass_1(act, step)

            def step(at):
                t3, t5 = at(3), at(5)
                if t5 is not None:
                    h = t5.slot(2)
                    act.wait_ge(S["hid_in_ps"], t5.n + 1)
                    a.activation(hid[:, h, :, :], hid_ps[h], ACT.Gelu).then_inc(S["hid_done"], 1)
                if t3 is not None:
                    h = t3.slot(2)
                    act.wait_ge(S["got_in_ps"], t3.n + 1)
                    a.copy(got_T[:, h, :], got_ps[h]).then_inc(S["got_T_done"], 1)
            pass_2(act, step)

        @block.vector
        def _(dve):
            v = nc.vector
            v.memset(bias3[:, :], 0.0).then_inc(S["bias_step"], 1)
            v.memset(ones_b[:, :], 1.0)
            v.memset(ones_h[:, :], 1.0)
            v.memset(v_sb[:, :, :, D:VW], 1.0)
            dve.wait_ge(S["bias_in"], 48)
            dve.wait_ge(S["bias_step"], 1)
            three = (0, 32, 64)
            for r in three:
                i = v.tensor_scalar_add(bias_f[r:r + 1, 0:2 * D], bias_f[r:r + 1, 0:2 * D], 1.0)
            i.then_inc(S["bias_step"], 1)
            dve.wait_ge(S["bias_step"], 2)
            v.tensor_copy(bias3[0:1, :], bias_f[0:1, :])
            for r in three[1:]:
                i = v.tensor_copy(bias_h[r:r + 1, :], bias_f[r:r + 1, :])
            i.then_inc(S["bias_step"], 1)
            dve.wait_ge(S["bias_step"], 3)
            for r in three[1:]:
                i = v.tensor_tensor(bias_r[r:r + 1, :], bias_f[r:r + 1, :], bias_h[r:r + 1, :], ALU.subtract)
            i.then_inc(S["bias_step"], 1)
            dve.wait_ge(S["bias_step"], 4)
            v.tensor_copy(bias3[32:33, :], bias_r[32:33, :])
            v.tensor_copy(bias_m[64:65, :], bias_r[64:65, :]).then_inc(S["bias_step"], 1)
            dve.wait_ge(S["bias_step"], 5)
            v.tensor_tensor(bias_s[64:65, :], bias_r[64:65, :], bias_m[64:65, :], ALU.subtract)\
             .then_inc(S["bias_step"], 1)
            dve.wait_ge(S["bias_step"], 6)
            v.tensor_copy(bias3[64:65, :], bias_s[64:65, :]).then_inc(S["dve_const"], 2)
            dve.wait_ge(S["affine_in"], 32)

            def stats(tag, b, out_stat, src):
                for t in range(TB):
                    i = v.bn_stats(out_stat[:, b.slot(2), t, :], src(t))
                i.then_inc(S[f"stats{tag}_done"], 1)

            def aggregate(tag, b, mv, stat):
                dve.wait_ge(S[f"stats{tag}_done"], b.n + 1)
                dve.sem_inc(S["passed_gate"], 1)
                for t in range(TB):
                    i = v.bn_aggr(mv[:, b.slot(2), t, :], stat[:, b.slot(2), t, :])
                i.then_inc(S[f"mv{tag}_done"], 1)

            def add_eps(tag, b, var, mv):
                dve.wait_ge(S[f"mv{tag}_done"], b.n + 1)
                v.tensor_scalar_add(var[:, b.slot(2), :], mv[:, b.slot(2), :, 1], LN_EPS)\
                 .then_inc(S[f"var{tag}_done"], 1)

            def per_expert(a):
                return a[:, :].unsqueeze(2).to_broadcast([P, PT, E])

            def step(u, at):
                b0, b1, b2, b3, b4 = at(0), at(1), at(2), at(3), at(4)
                closes = b4 is not None and b4.c % 2 == 1
                n = pair(b4) if closes else None
                half = (b4.c // 2) % 2 if closes else None
                if b0 is not None:
                    if isinstance(b0.n, int):
                        for c, (lo, _) in enumerate(X_CHUNKS):
                            if b0.n == lo:
                                dve.wait_ge(x_in[c], 16)
                    stats(1, b0, stat1, lambda t: x_tile(b0, t))
                    aggregate(1, b0, mv1, stat1)
                if b3 is not None:
                    dve.wait_ge(S["proj_in_ps"], b3.n + 1)
                    stats(2, b3, stat2, lambda t: proj_ps[:, t, :])
                if b0 is not None:
                    add_eps(1, b0, var1, mv1)
                if b3 is not None:
                    aggregate(2, b3, mv2, stat2)
                if b2 is not None:
                    h = b2.slot(2)
                    dve.wait_ge(S["sum_in_ps"], b2.n + 1)
                    v.tensor_tensor(kv_sb[:, h, :], sum_ps, head_mask[:, :], ALU.mult)\
                     .then_inc(S["kvsum_done"], 1)
                if b3 is not None:
                    add_eps(2, b3, var2, mv2)
                if closes:
                    dve.wait_ge(S["logits_in_ps"], b4.n + 1)
                    v.tensor_reduce(top1[:, :], logit_ps, AX.X, ALU.max).then_inc(S["top1_done"], 1)
                if b0 is not None:
                    h = b0.slot(2)
                    dve.wait_ge(S["rstd1_done"], b0.n + 1)
                    v.scalar_tensor_tensor(nb1[:, h, :], mv1[:, h, :, 0], -1.0, rstd1[:, h, :], ALU.mult, ALU.mult)
                    v.tensor_scalar_add(rp1[:, h, :], rstd1[:, h, :], 1.0).then_inc(S["nb1_done"], 1)
                if closes:
                    dve.wait_ge(S["top1_done"], n + 1)
                    v.tensor_tensor(is_top[:, :, :], logit_ps, per_expert(top1), ALU.is_equal)\
                     .then_inc(S["is_top_done"], 1)
                if b3 is not None:
                    h = b3.slot(2)
                    for t in range(TB):
                        i = v.scalar_tensor_tensor(scaled[:, h, t, :], proj_ps[:, t, :], mv2[:, h, t, 0:1],
                                                   gamma_b[:, :], ALU.subtract, ALU.mult)
                    i.then_inc(S["scaled_done"], 1)
                if closes:
                    if b4.least == 1:
                        dve.wait_ge(S["pool_const"], 5)
                    dve.wait_ge(S["is_top_done"], n + 1)
                    v.tensor_tensor(key[:, :, :], is_top[:, :, :], first_key[:, :, :], ALU.mult)\
                     .then_inc(S["key_done"], 1)
                if b3 is not None:
                    h = b3.slot(2)
                    dve.wait_ge(S["rstd2_done"], b3.n + 1)
                    dve.wait_ge(S["resid_done"], b3.n + 1)
                    dve.wait_ge(S["scaled_done"], b3.n + 1)
                    if b3.least >= UB:
                        dve.wait_ge(rows_free[(b3.c // 2) % 2], 16 * PT * b3.round())
                    for t in range(TB):
                        i = v.scalar_tensor_tensor(rows[:, b3.slot(UB), t, 0:D], scaled[:, h, t, :],
                                                   rstd2[:, h, t:t + 1], resid[:, b3.slot(UB), t, :],
                                                   ALU.mult, ALU.add)
                    i.then_inc(S["x1_done"], 1)
                if closes:
                    dve.wait_ge(S["key_done"], n + 1)
                    v.tensor_reduce(top_key[:, :], key[:, :, :], AX.X, ALU.max).then_inc(S["top_key_done"], 1)
                if b3 is not None:
                    dve.wait_ge(S["x1_done"], b3.n + 1)
                    stats(3, b3, stat3, lambda t: rows[:, b3.slot(UB), t, 0:D])
                if closes:
                    dve.wait_ge(S["top_key_done"], n + 1)
                    v.tensor_tensor(chosen[:, :, :], key[:, :, :], per_expert(top_key), ALU.is_equal)\
                     .then_inc(S["chosen_done"], 1)
                if b3 is not None:
                    aggregate(3, b3, mv3, stat3)
                if closes:
                    dve.wait_ge(S["chosen_done"], n + 1)
                    v.scalar_tensor_tensor(rest[:, :, :], chosen[:, :, :], NEG_HUGE, logit_ps, ALU.mult, ALU.add)\
                     .then_inc(S["rest_done"], 1)
                if b3 is not None:
                    add_eps(3, b3, var3, mv3)
                if b1 is not None:
                    h = b1.slot(2)
                    dve.wait_ge(S["v_done"], b1.n + 1)
                    v.scalar_tensor_tensor(phi_k[:, h, :, :], exp_k[:, h, :, :], 1.0, kv_ps[:, :, 0:D],
                                           ALU.min, ALU.max).then_inc(S["phik_done"], 1)
                if closes:
                    dve.wait_ge(S["rest_done"], n + 1)
                    v.tensor_reduce(top2[:, :], rest[:, :, :], AX.X, ALU.max).then_inc(S["top2_done"], 1)
                if b1 is not None:
                    h = b1.slot(2)
                    dve.wait_ge(S["expq_done"], b1.n + 1)
                    v.scalar_tensor_tensor(phi_q[:, h, :].rearrange("p (c r) -> p r c", r=R),
                                           exp_q[:, h, :].rearrange("p (r c) -> p r c", r=R), 1.0,
                                           q_ps.rearrange("p (r c) -> p r c", r=R), ALU.min, ALU.max)\
                     .then_inc(S["phiq_done"], 1)
                if closes:
                    dve.wait_ge(S["top2_done"], n + 1)
                    v.tensor_tensor(gap[:, :], top2[:, :], top1[:, :], ALU.subtract).then_inc(S["gap_done"], 1)
                    v.tensor_reduce(n_chosen[:, :], chosen[:, :, :].rearrange("p t e -> p e t"), AX.X, ALU.add)\
                     .then_inc(S["n_chosen_done"], 1)
                if b3 is not None:
                    h = b3.slot(2)
                    dve.wait_ge(S["rstd3_done"], b3.n + 1)
                    v.scalar_tensor_tensor(nb3[:, h, :], mv3[:, h, :, 0], -1.0, rows[:, b3.slot(UB), :, RSTD],
                                           ALU.mult, ALU.mult)
                    v.tensor_copy(rows[:, b3.slot(UB), :, MEAN], mv3[:, h, :, 0]).then_inc(S["nb3_done"], 1)
                if b2 is not None:
                    h = b2.slot(2)
                    dve.wait_ge(S["num_in_ps"], b2.n + 1)
                    v.tensor_scalar_max(den[:, h, :, :], num_ps[:, :, D:VW], DEN_MIN).then_inc(S["den_done"], 1)
                if closes:
                    dve.wait_ge(S["exp_gap_done"], n + 1)
                    v.tensor_scalar_add(gate_den[:, :], exp_gap[:, :], 1.0).then_inc(S["gate_den_done"], 1)
                if b2 is not None:
                    h = b2.slot(2)
                    dve.wait_ge(S["den_done"], b2.n + 1)
                    v.reciprocal(rden[:, h, :, :], den[:, h, :, :]).then_inc(S["rden_done"], 1)
                if closes:
                    dve.wait_ge(S["gate_den_done"], n + 1)
                    v.reciprocal(rows[:, 2 * half:2 * half + 2, :, GATE],
                                 gate_den[:, :].rearrange("p (b t) -> p b t", b=2))
                    dve.wait_ge(S["ranks_in_ps"], n + 1)
                    v.tensor_tensor(pos_sel[:, :, :], rank_ps, chosen[:, :, :], ALU.mult)\
                     .then_inc(S["pos_sel_done"], 1)
                    dve.wait_ge(S["n_chosen_done"], n + 1)
                    v.tensor_tensor(seen[:, :], seen[:, :], n_chosen[:, :], ALU.add).then_inc(S["seen_done"], 1)
                if b2 is not None:
                    h = b2.slot(2)
                    dve.wait_ge(S["rden_done"], b2.n + 1)
                    v.tensor_tensor(attn[:, h, :, :].rearrange("p d (t g) -> p t g d", t=TB),
                                    num_ps[:, :, 0:D].rearrange("p t (g d) -> p t g d", g=HEADS),
                                    rden[:, h, :, :].unsqueeze(3).to_broadcast([P, TB, HEADS, HD]),
                                    ALU.mult).then_inc(S["attn_done"], 1)
                if closes:
                    dve.wait_ge(S["pos_sel_done"], n + 1)
                    with nc.allow_low_precision("row numbers are whole and below 2^24"):
                        v.tensor_reduce(pos[:, half, :], pos_sel[:, :, :], AX.X, ALU.add)\
                         .then_inc(S["pos_done"], 1)
                if b2 is not None:
                    h = b2.slot(2)
                    dve.wait_ge(S["attn_done"], b2.n + 1)
                    v.transpose(regrouped[:, h, :, :, :].rearrange("p a d r -> p d a r"),
                                attn[:, h, :, :]).then_inc(S["regrouped_done"], 1)

            dve.wait_ge(S["pool_const"], 4)
            pass_1(dve, step)

            count = [0]

            def link(ins):
                count[0] += 1
                ins.then_inc(S["table_step"], 1)
                dve.wait_ge(S["table_step"], count[0])
            v.memset(reached[:, :, 0:1], 1.0)
            dve.wait_ge(S["counts_in_ps"], 1)
            link(v.tensor_tensor(n_tok[:, :], count_ps, region_base[:, :], ALU.subtract))
            link(v.tensor_tensor(over[:, :, :], n_tok[:, :].unsqueeze(2).to_broadcast([P, E, TOK // P]),
                                 step_128[:, :, :], ALU.is_gt))
            link(v.tensor_reduce(n_tiles[:, :], over[:, :, :], AX.X, ALU.add))
            link(v.tensor_tensor(tiles_m[:, :, :], n_tiles[:, :].unsqueeze(1).to_broadcast([P, E, E]),
                                 upto[:, :, :], ALU.mult))
            link(v.tensor_reduce(tiles_upto[:, :], tiles_m[:, :, :], AX.X, ALU.add))
            v.tensor_tensor(reached[:, :, 1:E + 1], tile_no[:, :].unsqueeze(2).to_broadcast([P, NT, E]),
                            tiles_upto[:, :].unsqueeze(1).to_broadcast([P, NT, E]), ALU.is_ge)
            link(v.tensor_tensor(tiles_before[:, :], tiles_upto[:, :], n_tiles[:, :], ALU.subtract))
            v.tensor_tensor(mine[:, :, :], reached[:, :, 0:E], reached[:, :, 1:E + 1], ALU.subtract)
            link(v.scalar_tensor_tensor(row_base[:, :], tiles_before[:, :], float(P), count_ps, ALU.mult, ALU.add))
            link(v.tensor_tensor(row_of[:, :, :], row_base[:, :].unsqueeze(1).to_broadcast([P, NT, E]),
                                 tile_end[:, :].unsqueeze(2).to_broadcast([P, NT, E]), ALU.subtract))
            v.tensor_reduce(passed[:, :], reached[:, :, 1:E + 1], AX.X, ALU.add)
            link(v.tensor_tensor(row_sel[:, :, :], row_of[:, :, :], mine[:, :, :], ALU.mult))
            v.tensor_scalar_min(tile_expert[:, :], passed[:, :], float(E - 1))
            with nc.allow_low_precision("row numbers are whole and below 2^24"):
                v.tensor_reduce(tile_row[:, :], row_sel[:, :, :], AX.X, ALU.add).then_inc(S["table_done"], 1)
            dve.wait_ge(S["table_done"], 1)
            dve.wait_ge(S["ffn_in"], 32)

            def step(at):
                t2, t3, t5 = at(2), at(3), at(5)
                if t3 is not None:
                    h = t3.slot(2)
                    expert = dve.value_load(tile_expert[0:1, bass.ds(t3.n, 1)], min_val=0, max_val=E - 1)
                    if t3.least >= 2:
                        dve.wait_ge(S["hid_in_ps"], t3.n - 1)
                    v.tensor_copy(w1_tile[:, h, :], w1_sb[:, bass.ds(expert * HID, HID)])\
                     .then_inc(S["w1_tile_done"], 1)
                if t2 is not None:
                    h = t2.slot(2)
                    s = t2.slot(UT)
                    dve.wait_ge(got_in[s], 16 * (t2.round() + 1))
                    if t2.least >= 2:
                        dve.wait_ge(S["got_in_ps"], t2.n - 1)
                    v.tensor_scalar(got_n[:, h, :], got[:, s, 0:D], got[:, s, MEAN:MEAN + 1],
                                    got[:, s, RSTD:RSTD + 1], ALU.subtract, ALU.mult).then_inc(S["got_n_done"], 1)
                if t5 is not None:
                    h = t5.slot(2)
                    s = t5.slot(UT)
                    dve.wait_ge(S["y_in_ps"], t5.n + 1)
                    if t5.least >= UT:
                        dve.wait_ge(out_done[s], 16 * t5.round())
                    v.tensor_copy(done_token[:, s:s + 1], got[:, s, TOKEN:TOKEN + 1].bitcast(I32))
                    v.scalar_tensor_tensor(done[:, s, :], y_ps[h], got[:, s, GATE:GATE + 1], got[:, s, 0:D],
                                           ALU.mult, ALU.add).then_inc(S["done_ready"], 1)
            pass_2(dve, step)


def kernel(L0_attn_H, L0_attn_W_qkv, L0_attn_b_qkv, L0_attn_W_proj, L0_attn_b_proj, L0_attn_gamma,
           L0_attn_beta, L0_ffn_Wr, L0_ffn_W1, L0_ffn_W2):
    import numpy as np
    import concourse.bacc as bacc
    from concourse.bass_utils import run_bass_kernel_spmd as run

    H = np.asarray(L0_attn_H)
    B, N, D = H.shape
    W1, W2 = np.asarray(L0_ffn_W1), np.asarray(L0_ffn_W2)
    E, _, HID = W1.shape
    bias = np.concatenate([np.asarray(L0_attn_b_qkv), np.asarray(L0_attn_b_proj)])
    split = (B, 16, 2, 4, 2, D)
    x = H.reshape(split).transpose(3, 2, 1, 0, 4, 5).reshape(128, B, 2 * D)
    wproj_t = np.asarray(L0_attn_W_proj).T.reshape(2, 4, 2, 8, D).transpose(3, 2, 1, 0, 4).reshape(D, D)
    arrays = {
        "x": x,
        "wqkv_t": np.asarray(L0_attn_W_qkv).T,
        "b_all": np.broadcast_to(bias, (3, bias.size)),
        "wproj_t": wproj_t,
        "gamma": np.asarray(L0_attn_gamma),
        "beta": np.asarray(L0_attn_beta),
        "w_router": np.asarray(L0_ffn_Wr),
        "w1": W1.transpose(1, 0, 2).reshape(D, E * HID),
        "w2": W2.reshape(E, HID // 128, 128, D).transpose(2, 0, 1, 3).reshape(128, E * HID),
    }
    arrays = {k: np.ascontiguousarray(a) for k, a in arrays.items()}
    nc = bacc.Bacc("TRN2", target_bir_lowering=False, num_devices=1)
    args = [nc.dram_tensor(k, a.shape, F32, kind="ExternalInput").ap() for k, a in arrays.items()]
    args.append(nc.dram_tensor("out", [B * N, D], F32, kind="ExternalOutput").ap())
    build(nc, *args)
    r = run(nc, [arrays], core_ids=[0])
    return r.results[0]["out"].reshape(B, 4, 2, 16, 2, D).transpose(0, 3, 2, 1, 4, 5).reshape(H.shape)
```

```python
from contextlib import ExitStack

import concourse.bass as bass
from concourse import mybir

ALU = mybir.AluOpType
ACT = mybir.ActivationFunctionType
AX = mybir.AxisListType
F32 = mybir.dt.float32
F16 = mybir.dt.float16
BF16 = mybir.dt.bfloat16
I32 = mybir.dt.int32

P = 128
LN_EPS = 1e-5
DEN_MIN = 1e-6
NEG_HUGE = -3.0e38


class Item:

    def __init__(self, unroll, j, c, j_min=0):
        self.unroll, self.j, self.c = unroll, j, c
        self.n = unroll * j + c
        self.least = unroll * (j if isinstance(j, int) else j_min) + c

    def slot(self, k):
        return self.c % k

    def round(self):
        return self.j + self.c // self.unroll

    def least_round(self):
        return self.least // self.unroll


def build(nc, x, wqkv_t, b_all, wproj_t, gamma, beta, w_router, w1, w2, out):
    D = wproj_t.shape[0]
    TOK = x.shape[0] * x.shape[1] * x.shape[2] // D
    E = w_router.shape[1]
    HID = w1.shape[1] // E
    HEADS = 16
    HD = D // HEADS
    CH = HID // P
    TB = 2
    SEQ = TB * P
    NB = TOK // SEQ
    VW = D + HEADS
    UB = 4
    PT = 2 * TB
    REGION = TOK + P
    ROW = D + 4
    MEAN, RSTD, GATE, TOKEN = D, D + 1, D + 2, D + 3
    NT = TOK // P + E - 1
    UT = 6
    LAG_B, LAG_T = 7, 5
    assert D == P and NB % UB == 0 and HID % P == 0

    R = SEQ // HEADS
    assert R == HEADS == 16
    rows_dram = nc.dram_tensor("expert_rows", [E * REGION, ROW], F32, kind="Internal").ap()

    with ExitStack() as ctx:
        def sb(name, shape, dt=F32):
            return ctx.enter_context(nc.sbuf_tensor(name, shape, dt))

        def ps(name, shape):
            return ctx.enter_context(nc.psum_tensor(name, shape, F32))

        def sem(name):
            return ctx.enter_context(nc.semaphore(name))

        wqkv = sb("wqkv", [P, 3 * D])
        wproj = sb("wproj", [P, D])
        wproj_mean = sb("wproj_mean", [P, 1])
        wproj2 = sb("wproj2", [P, 2, D])
        wr = sb("wr", [P, E])
        wr_c = sb("wr_c", [P, E])
        w1_sb = sb("w1_sb", [P, E * HID])
        w2_sb = sb("w2_sb", [P, E * HID])
        gamma_b = sb("gamma_b", [P, D])
        beta_b = sb("beta_b", [P, D])
        bias_f = sb("bias_f", [P, 5 * D])
        bias_mean = sb("bias_mean", [P, 1])
        bias_r = sb("bias_r", [P, 5 * D])
        bias_s = sb("bias_s", [P, 5 * D])
        bias3 = sb("bias3", [P, 5 * D], BF16)
        bias_h = sb("bias_h", [P, 5 * D], BF16)
        bias_m = sb("bias_m", [P, 5 * D], BF16)
        ones_b = sb("ones_b", [P, SEQ], BF16)
        ones_h = sb("ones_h", [P, P], F16)
        before = sb("before", [P, P], F16)
        ident = sb("ident", [P, P])
        averaging = sb("averaging", [P, P])
        head_mask = sb("head_mask", [P, VW])
        neg_half = sb("neg_half", [P, TB])
        first_key = sb("first_key", [P, PT, E])
        token_no = sb("token_no", [P, NB * TB], I32)
        region_base = sb("region_base", [P, E])
        step_128 = sb("step_128", [P, E, TOK // P])
        upto = sb("upto", [P, E, E])
        tile_no = sb("tile_no", [P, NT])
        tile_end = sb("tile_end", [P, NT])
        pad_rows = sb("pad_rows", [P, ROW])

        x_sb = sb("x_sb", [P, NB, SEQ])
        stat1 = sb("stat1", [P, 2, TB, 6])
        mv1 = sb("mv1", [P, 2, TB, 2])
        var1 = sb("var1", [P, 2, TB])
        rstd1 = sb("rstd1", [P, 2, TB])
        nb1 = sb("nb1", [P, 2, TB])
        rp1 = sb("rp1", [P, 2, TB])
        xn = sb("xn", [P, 2, TB, D])
        xx = sb("xx", [P, 2, TB, D])
        resid = sb("resid", [P, UB, TB, D])
        xnT = sb("xnT", [P, 2, SEQ])
        exp_q = sb("exp_q", [P, 2, SEQ])
        exp_k = sb("exp_k", [P, 2, TB, D])
        phi_q = sb("phi_q", [P, 2, SEQ])
        phi_k = sb("phi_k", [P, 2, TB, D])
        v_sb = sb("v_sb", [P, 2, TB, VW])
        kv_sb = sb("kv_sb", [P, 2, VW])
        den = sb("den", [P, 2, TB, HEADS])
        rden = sb("rden", [P, 2, TB, HEADS])
        attn = sb("attn", [P, 2, HD, 2 * HEADS])
        regrouped = sb("regrouped", [P, 2, TB, HD, R])
        turned = sb("turned", [P, 2, 2, SEQ])
        var2 = sb("var2", [P, 2, TB])
        squares = sb("squares", [P, 2, TB, D], BF16)
        sumsq = sb("sumsq", [P, 2, TB])
        rstd2 = sb("rstd2", [P, 2, TB])
        rows = sb("rows", [P, UB, TB, ROW])
        stat3 = sb("stat3", [P, 2, TB, 6])
        var3 = sb("var3", [P, 2, TB])
        top1 = sb("top1", [P, PT])
        is_top = sb("is_top", [P, PT, E])
        key = sb("key", [P, PT, E])
        top_key = sb("top_key", [P, PT])
        chosen = sb("chosen", [P, PT, E], F16)
        rest = sb("rest", [P, PT, E])
        top2 = sb("top2", [P, PT])
        diff = sb("diff", [P, PT])
        gap = sb("gap", [P, PT])
        exp_gap = sb("exp_gap", [P, PT])
        gate_den = sb("gate_den", [P, PT])
        n_chosen = sb("n_chosen", [P, E])
        seen = sb("seen", [P, E], F16)
        pos_sel = sb("pos_sel", [P, PT, E])
        pos = sb("pos", [P, 2, PT], I32)
        n_tok = sb("n_tok", [P, E])
        over = sb("over", [P, E, TOK // P])
        n_tiles = sb("n_tiles", [P, E])
        tiles_m = sb("tiles_m", [P, E, E])
        tiles_upto = sb("tiles_upto", [P, E])
        tiles_before = sb("tiles_before", [P, E])
        row_base = sb("row_base", [P, E])
        reached = sb("reached", [P, NT, E + 1])
        mine = sb("mine", [P, NT, E])
        row_of = sb("row_of", [P, NT, E])
        row_sel = sb("row_sel", [P, NT, E])
        passed = sb("passed", [P, NT])
        tile_row = sb("tile_row", [P, NT], I32)
        tile_expert = sb("tile_expert", [P, NT], I32)

        got = sb("got", [P, UT, ROW])
        got_n = sb("got_n", [P, 2, D])
        got_T = sb("got_T", [P, 2, P])
        w1_tile = sb("w1_tile", [P, 2, HID])
        hid = sb("hid", [P, 2, CH, P])
        done = sb("done", [P, UT, D])
        done_token = sb("done_token", [P, UT], I32)

        bank = [ps(f"bank{i}", [P, 512]) for i in range(8)]
        xnT_ps = bank[0][:, 0:SEQ]
        turned_ps = bank[1][:, :].rearrange("p (k c) -> p k c", k=2)
        sum_ps = bank[2][:, 0:VW]
        q_ps = bank[3][:, 0:SEQ]
        kv_ps = bank[4][:, :].rearrange("p (t c) -> p t c", t=TB)
        num_ps = bank[5][:, 0:TB * VW].rearrange("p (t c) -> p t c", t=TB)
        proj_ps = bank[6][:, :].rearrange("p (t k c) -> p t k c", t=TB, k=2)
        logit_ps = bank[7][:, 0:PT * E].rearrange("p (t e) -> p t e", t=PT)
        rank_ps = bank[7][:, 64:64 + PT * E].rearrange("p (t e) -> p t e", t=PT)
        count_ps = bank[7][:, 128:128 + E]
        wr_mean_ps = bank[7][:, 136:136 + E]
        got_ps = [bank[0 + h][:, 0:P] for h in range(2)]
        hid_ps = [bank[2 + h][:, :].rearrange("p (c t) -> p c t", c=CH) for h in range(2)]
        y_ps = [bank[4 + h][:, 0:D] for h in range(2)]

        S = {n: sem(n) for n in (
            "weights_in", "bias_in", "affine_in", "ffn_in", "pads_in",
            "pool_const", "dve_const", "bias_step", "proj_step", "proj_const", "router_mean_in_ps",
            "router_const", "mask_step",
            "stats1_done", "mv1_done", "var1_done", "rstd1_done", "nb1_done", "xn_done", "xx_done",
            "resid_done", "xnT_in_ps", "xnT_done", "q_in_ps", "kv_in_ps", "expk_done", "v_done",
            "expq_done", "phik_done", "phiq_done", "sum_in_ps", "kvsum_done", "num_in_ps",
            "den_done", "rden_done", "attn_done", "regrouped_done", "turned_in_ps", "turned_done",
            "proj_in_ps", "sumsq_done", "var2_done", "rstd2_done", "x1_done",
            "stats3_done", "mv3_done", "var3_done", "rstd3_done",
            "logits_in_ps", "top1_done", "is_top_done", "key_done",
            "top_key_done", "chosen_done", "rest_done", "top2_done", "diff_done", "gap_done",
            "exp_gap_done", "gate_den_done", "n_chosen_done", "ranks_in_ps", "pos_sel_done",
            "seen_done", "pos_done", "token_done", "counts_in_ps", "table_step", "table_done",
            "got_n_done", "got_in_ps", "got_T_done", "w1_tile_done", "hid_in_ps", "hid_done",
            "y_in_ps", "done_ready", "passed_gate")}
        x_in = [sem(f"x_in{c}") for c in range(4)]
        rows_free = [sem(f"rows_free{h}") for h in range(UB)]
        got_in = [sem(f"got_in{h}") for h in range(UT)]
        out_done = [sem(f"out_done{h}") for h in range(UT)]

        X_CHUNKS = [(0, 1), (1, 2), (2, 4), (4, NB)]

        def pass_1(eng, step):
            def peeled(s):
                def at(lag):
                    return Item(UB, (s - lag) // UB, (s - lag) % UB) if 0 <= s - lag < NB else None
                step(s % UB, at)
            first = 2 * UB
            for s in range(first):
                peeled(s)
            with eng.Fori(first // UB, NB // UB) as j:
                for u in range(UB):
                    step(u, lambda lag: Item(UB, j, u - lag, first // UB))
            for s in range(NB, NB + LAG_B):
                peeled(s)

        def pass_2(eng, step):
            def peeled(s):
                def at(lag):
                    return Item(UT, (s - lag) // UT, (s - lag) % UT) if 0 <= s - lag < NT else None
                step(at)
            first = 2 * UT
            for s in range(first):
                peeled(s)
            with eng.Fori(first // UT, NT // UT) as j:
                for u in range(UT):
                    step(lambda lag: Item(UT, j, u - lag, first // UT))
            for s in range(NT // UT * UT, NT + LAG_T):
                peeled(s)

        def pair(b):
            return UB // 2 * b.j + b.c // 2

        def x_tile(b, t):
            return x_sb[:, bass.ds(b.n, 1), t * D:t * D + D].rearrange("p a d -> p (a d)")

        block = ctx.enter_context(nc.Block())

        @block.sync
        def _(sp):
            def load_x(c):
                lo, hi = X_CHUNKS[c]
                sp.dma_start(x_sb[:, lo:hi, :], x[:, lo:hi, :]).then_inc(x_in[c], 16)
            load_x(0)
            sp.dma_start(wqkv[:, :], wqkv_t).then_inc(S["weights_in"], 16)
            load_x(1)
            load_x(2)
            sp.dma_start(wproj[:, :], wproj_t).then_inc(S["weights_in"], 16)
            sp.dma_start(wr[:, :], w_router).then_inc(S["weights_in"], 16)
            load_x(3)
            sp.dma_start(w1_sb[:, :], w1).then_inc(S["ffn_in"], 16)
            sp.dma_start(w2_sb[:, :], w2).then_inc(S["ffn_in"], 16)
            sp.wait_ge(S["pool_const"], 1)
            sp.dma_start(rows_dram.rearrange("(e r) c -> r e c", e=E)[0:P],
                         pad_rows[:, :].unsqueeze(1).to_broadcast([P, E, ROW])).then_inc(S["pads_in"], 16)

            sp.wait_ge(S["table_done"], 1)
            sp.wait_ge(S["pads_in"], 16)
            for h in range(UB):
                sp.wait_ge(rows_free[h], 16 * TB * (NB // UB))

            def step(at):
                t = at(0)
                if t is not None:
                    row = sp.value_load(tile_row[0:1, bass.ds(t.n, 1)], min_val=0, max_val=E * REGION - P)
                    if t.least >= UT:
                        sp.wait_ge(S["done_ready"], t.n - UT + 1)
                    sp.dma_start(got[:, t.slot(UT), :], rows_dram[bass.ds(row, P), :])\
                      .then_inc(got_in[t.slot(UT)], 16)
            pass_2(sp, step)
            for h in range(UT):
                sp.wait_ge(out_done[h], 16 * ((NT - 1 - h) // UT + 1))

        @block.gpsimd
        def _(pool):
            g = nc.gpsimd
            g.memset(pad_rows[:, :], 0.0).then_inc(S["mask_step"], 1)
            pool.wait_ge(S["mask_step"], 1)
            g.iota(pad_rows[:, TOKEN:TOKEN + 1].bitcast(I32), pattern=[[1, 1]], base=TOK,
                   channel_multiplier=1).then_inc(S["pool_const"], 1)
            g.memset(neg_half[:, :], -0.5)
            g.memset(averaging[:, :], 1.0 / P)
            g.memset(ident[:, :], 0.0).then_inc(S["mask_step"], 1)
            pool.wait_ge(S["mask_step"], 2)
            g.affine_select(out=ident[:, :], in_=ident[:, :], compare_op=ALU.not_equal, fill=1.0,
                            base=0, pattern=[[-1, P]], channel_multiplier=1).then_inc(S["pool_const"], 1)
            g.memset(head_mask[:, :], 1.0).then_inc(S["mask_step"], 1)
            pool.wait_ge(S["mask_step"], 3)
            parts = [(head_mask[:, 0:D], [[-HD, HEADS], [0, HD]]), (head_mask[:, D:VW], [[-HD, HEADS]])]
            for m, pat in parts:
                g.affine_select(out=m, in_=m, compare_op=ALU.is_ge, fill=0.0, base=0, pattern=pat,
                                channel_multiplier=1).then_inc(S["mask_step"], 1)
            pool.wait_ge(S["mask_step"], 5)
            for m, pat in parts:
                g.affine_select(out=m, in_=m, compare_op=ALU.is_ge, fill=0.0, base=HD - 1,
                                pattern=[[-a, n] for a, n in pat], channel_multiplier=-1)\
                 .then_inc(S["pool_const"], 1)

            def more_constants():
                g.memset(before[:, :], 1.0).then_inc(S["mask_step"], 1)
                g.memset(upto[:, :, :], 1.0).then_inc(S["mask_step"], 1)
                pool.wait_ge(S["mask_step"], 7)
                g.affine_select(out=before[:, :], in_=before[:, :], compare_op=ALU.is_gt, fill=0.0, base=0,
                                pattern=[[1, P]], channel_multiplier=-1)
                g.affine_select(out=upto[:, :, :], in_=upto[:, :, :], compare_op=ALU.is_ge, fill=0.0,
                                base=0, pattern=[[1, E], [-1, E]], channel_multiplier=0)
                g.iota(first_key[:, :, :], pattern=[[0, PT], [-1, E]], base=E, channel_multiplier=0,
                       allow_small_or_imprecise_dtypes=True)
                g.iota(seen[:, :], pattern=[[REGION // P, E]], base=1, channel_multiplier=0,
                       allow_small_or_imprecise_dtypes=True)
                g.iota(token_no[:, :].rearrange("p (b t) -> p b t", t=TB), pattern=[[SEQ, NB], [1, TB]],
                       base=0, channel_multiplier=TB)
                g.iota(region_base[:, :], pattern=[[REGION, E]], base=P, channel_multiplier=0,
                       allow_small_or_imprecise_dtypes=True)
                g.iota(step_128[:, :, :], pattern=[[0, E], [P, TOK // P]], base=0, channel_multiplier=0,
                       allow_small_or_imprecise_dtypes=True)
                g.iota(tile_no[:, :], pattern=[[1, NT]], base=0, channel_multiplier=0,
                       allow_small_or_imprecise_dtypes=True)
                g.iota(tile_end[:, :], pattern=[[P, NT]], base=P, channel_multiplier=0,
                       allow_small_or_imprecise_dtypes=True).then_inc(S["pool_const"], 1)

            pool.wait_ge(S["affine_in"], 32)

            def scatter(b, last, tile):
                g.indirect_dma_start(
                    out=rows_dram, in_=rows[:, (b.c - (not last)) % UB, tile, :],
                    out_offset=bass.IndirectOffsetOnAxis(
                        ap=pos[:, (b.c // 2) % 2, TB * last + tile:TB * last + tile + 1], axis=0),
                    in_offset=None, bounds_check=E * REGION - 1, oob_is_err=False)\
                 .then_inc(rows_free[(b.c - (not last)) % UB], 16)

            def step(u, at):
                b0, b4, b6, b7 = at(0), at(4), at(6), at(7)
                if b4 is not None:
                    h = b4.slot(2)
                    pool.wait_ge(S["var2_done"], b4.n + 1)
                    g.tensor_tensor(rstd2[:, h, :], var2[:, h, :], neg_half[:, :], ALU.pow)\
                     .then_inc(S["rstd2_done"], 1)
                going = next(((b, last) for b, last in ((b6, 0), (b7, 1))
                              if b is not None and b.c % 2 == 1), None)
                if going and not going[1]:
                    pool.wait_ge(S["pos_done"], pair(b6) + 1)
                    pool.wait_ge(S["token_done"], b6.n + 1)
                    pool.wait_ge(S["rstd3_done"], b6.n + 1)
                    pool.sem_inc(S["passed_gate"], 1)
                if going:
                    scatter(*going, 0)
                if b0 is not None:
                    h = b0.slot(2)
                    pool.wait_ge(S["var1_done"], b0.n + 1)
                    g.tensor_tensor(rstd1[:, h, :], var1[:, h, :], neg_half[:, :], ALU.pow)\
                     .then_inc(S["rstd1_done"], 1)
                if b0 is not None and b0.least == 0:
                    more_constants()
                if going:
                    scatter(*going, 1)
                if b4 is not None:
                    h = b4.slot(2)
                    pool.wait_ge(S["var3_done"], b4.n + 1)
                    g.tensor_tensor(rows[:, b4.slot(UB), :, RSTD], var3[:, h, :], neg_half[:, :], ALU.pow)\
                     .then_inc(S["rstd3_done"], 1)
                    g.tensor_copy(rows[:, b4.slot(UB), :, TOKEN].bitcast(I32),
                                  token_no[:, bass.ds(TB * b4.n, TB)]).then_inc(S["token_done"], 1)
                if b0 is not None:
                    h = b0.slot(2)
                    pool.wait_ge(S["xx_done"], b0.n + 1)
                    g.tensor_tensor(resid[:, b0.slot(UB), :, :], xx[:, h, :, :],
                                    beta_b[:, :].unsqueeze(1).to_broadcast([P, TB, D]), ALU.add)\
                     .then_inc(S["resid_done"], 1)
            pass_1(pool, step)

            def step(at):
                t = at(5)
                if t is not None:
                    pool.wait_ge(S["done_ready"], t.n + 1)
                    pool.sem_inc(S["passed_gate"], 1)
                    g.indirect_dma_start(
                        out=out, out_offset=bass.IndirectOffsetOnAxis(
                            ap=done_token[:, t.slot(UT):t.slot(UT) + 1], axis=0),
                        in_=done[:, t.slot(UT), :], in_offset=None, bounds_check=TOK - 1, oob_is_err=False).then_inc(out_done[t.slot(UT)], 16)
            pass_2(pool, step)

        @block.tensor
        def _(pe):
            t_ = nc.tensor
            pe.wait_ge(S["pool_const"], 4)
            pe.wait_ge(S["dve_const"], 2)

            def step(u, at):
                b1, b2, b3, b4, b5 = at(1), at(2), at(3), at(4), at(5)
                if b1 is not None:
                    h = b1.slot(2)
                    pe.wait_ge(S["xn_done"], b1.n + 1)
                    for t in range(TB):
                        mm = t_.transpose(xnT_ps[:, P * t:P * t + P], xn[:, h, t, :], ident[:, :])
                    mm.then_inc(S["xnT_in_ps"], 1)
                if b2 is not None:
                    h = b2.slot(2)
                    pe.wait_ge(S["phik_done"], b2.n + 1)
                    pe.wait_ge(S["v_done"], b2.n + 1)
                    for t in range(TB):
                        mm = t_.matmul(sum_ps, phi_k[:, h, t, :], v_sb[:, h, t, :],
                                       start=t == 0, stop=t == TB - 1)
                    mm.then_inc(S["sum_in_ps"], 1)
                if b1 is not None:
                    h = b1.slot(2)
                    if b1.least == 0:
                        t_.matmul(wr_mean_ps, averaging[:, :], wr[:, :], start=True, stop=True)\
                          .then_inc(S["router_mean_in_ps"], 1)
                    pe.wait_ge(S["xnT_done"], b1.n + 1)
                    for t in range(TB):
                        t_.matmul(kv_ps[:, t, :], ones_b[:, 0:P], bias3[:, D:3 * D], start=True, stop=False)
                        mm = t_.matmul(kv_ps[:, t, :], xnT[:, h, P * t:P * t + P], wqkv[:, D:3 * D],
                                       start=False, stop=True)
                    mm.then_inc(S["kv_in_ps"], 1)
                    if b1.least >= 1:
                        pe.wait_ge(S["phiq_done"], b1.n)
                    t_.matmul(q_ps, bias3[:, 0:D], ones_b[:, :], start=True, stop=False)
                    t_.matmul(q_ps, wqkv[:, 0:D], xnT[:, h, :], start=False, stop=True)\
                      .then_inc(S["q_in_ps"], 1)
                if b4 is not None:
                    pe.wait_ge(S["x1_done"], b4.n + 1)
                    for t in range(TB):
                        mm = t_.transpose(turned_ps[:, 0, P * t:P * t + P], rows[:, b4.slot(UB), t, 0:D], ident[:, :])
                if b3 is not None:
                    h = b3.slot(2)
                    pe.wait_ge(S["regrouped_done"], b3.n + 1)
                    for t in range(TB):
                        mm = t_.transpose(turned_ps[:, 1, P * t:P * t + P],
                                          regrouped[:, h, t, :, :].rearrange("p d r -> p (d r)"), ident[:, :])
                if b3 is not None or b4 is not None:
                    mm.then_inc(S["turned_in_ps"], 1)
                if b2 is not None:
                    h = b2.slot(2)
                    pe.wait_ge(S["kvsum_done"], b2.n + 1)
                    pe.wait_ge(S["phiq_done"], b2.n + 1)
                    for t in range(TB):
                        mm = t_.matmul(num_ps[:, t, :], phi_q[:, h, P * t:P * t + P], kv_sb[:, h, :],
                                       start=True, stop=True)
                    mm.then_inc(S["num_in_ps"], 1)
                if b5 is not None and b5.c % 2 == 1:
                    n = pair(b5)
                    if b5.least == 1:
                        pe.wait_ge(S["pool_const"], 5)
                    pe.wait_ge(S["rest_done"], n + 1)
                    if b5.least >= 2:
                        pe.wait_ge(S["seen_done"], n)
                    t_.matmul(rank_ps, ones_h[:, :], seen[:, :].unsqueeze(1).to_broadcast([P, PT, E]),
                              start=True, stop=False)
                    for t in range(PT - 1):
                        t_.matmul(rank_ps[:, t + 1:PT, :], ones_h[:, :],
                                  chosen[:, t:t + 1, :].to_broadcast([P, PT - 1 - t, E]),
                                  start=False, stop=False)
                    t_.matmul(rank_ps, before[:, :], chosen[:, :, :], start=False, stop=True)\
                      .then_inc(S["ranks_in_ps"], 1)
                if b3 is not None:
                    h = b3.slot(2)
                    pe.wait_ge(S["turned_done"], b3.n + 1)
                    if b3.least == 0:
                        pe.wait_ge(S["proj_const"], 2)
                    for t in range(TB):
                        t_.matmul(proj_ps[:, t, :, :], ones_b[:, 0:P], bias3[:, 3 * D:5 * D], start=True, stop=False)
                        mm = t_.matmul(proj_ps[:, t, :, :], turned[:, h, 1, P * t:P * t + P], wproj2[:, :, :],
                                       start=False, stop=True)
                    mm.then_inc(S["proj_in_ps"], 1)
                if b4 is not None:
                    h = b4.slot(2)
                    pe.wait_ge(S["turned_done"], b4.n + 2)
                    if b4.least == 0:
                        pe.wait_ge(S["router_const"], 1)
                    if b4.c % 2 == 0 and b4.least >= 2:
                        pe.wait_ge(S["pos_sel_done"], pair(b4))
                    for t in range(TB):
                        mm = t_.matmul(logit_ps[:, TB * h + t, :], turned[:, (b4.c + 1) % 2, 0, P * t:P * t + P], wr_c[:, :],
                                       start=True, stop=True)
                    mm.then_inc(S["logits_in_ps"], 1)

            pe.wait_ge(S["weights_in"], 48)
            pass_1(pe, step)
            pe.wait_ge(S["seen_done"], NB // 2)
            t_.matmul(count_ps, ones_h[:, :], seen[:, :], start=True, stop=True).then_inc(S["counts_in_ps"], 1)

            pe.wait_ge(S["ffn_in"], 32)
            pe.wait_ge(S["table_done"], 1)

            def step(at):
                t3, t4, t5 = at(3), at(4), at(5)
                if t3 is not None:
                    h = t3.slot(2)
                    pe.wait_ge(S["got_n_done"], t3.n + 1)
                    t_.transpose(got_ps[h], got_n[:, h, :], ident[:, :]).then_inc(S["got_in_ps"], 1)
                if t4 is not None:
                    h = t4.slot(2)
                    pe.wait_ge(S["got_T_done"], t4.n + 1)
                    pe.wait_ge(S["w1_tile_done"], t4.n + 1)
                    for c in range(CH):
                        mm = t_.matmul(hid_ps[h][:, c, :], w1_tile[:, h, P * c:P * c + P], got_T[:, h, :],
                                       start=True, stop=True)
                    mm.then_inc(S["hid_in_ps"], 1)
                if t5 is not None:
                    h = t5.slot(2)
                    expert = pe.value_load(tile_expert[0:1, bass.ds(t5.n, 1)], min_val=0, max_val=E - 1)
                    pe.wait_ge(S["hid_done"], t5.n + 1)
                    if t5.least >= 2:
                        pe.wait_ge(S["done_ready"], t5.n - 1)
                    for c in range(CH):
                        mm = t_.matmul(y_ps[h], hid[:, h, c, :], w2_sb[:, bass.ds(expert * HID + P * c, P)],
                                       start=c == 0, stop=c == CH - 1)
                    mm.then_inc(S["y_in_ps"], 1)
            pass_2(pe, step)

        @block.scalar
        def _(act):
            a = nc.scalar
            for r in range(3):
                act.dma_start(bias_f[32 * r:32 * r + 1, 0:4 * D], b_all[r:r + 1, :]).then_inc(S["bias_in"], 16)
            act.dma_start(gamma_b[:, :], gamma.partition_broadcast(P)).then_inc(S["affine_in"], 16)
            act.dma_start(beta_b[:, :], beta.partition_broadcast(P)).then_inc(S["affine_in"], 16)

            def step(u, at):
                b0, b1, b3, b4, b5 = at(0), at(1), at(3), at(4), at(5)
                if b1 is not None:
                    h = b1.slot(2)
                    act.wait_ge(S["xnT_in_ps"], b1.n + 1)
                    a.copy(xnT[:, h, :], xnT_ps).then_inc(S["xnT_done"], 1)
                    act.wait_ge(S["kv_in_ps"], b1.n + 1)
                    a.activation(exp_k[:, h, :, :], kv_ps[:, :, 0:D], ACT.Exp, bias=-1.0).then_inc(S["expk_done"], 1)
                    a.copy(v_sb[:, h, :, 0:D], kv_ps[:, :, D:2 * D]).then_inc(S["v_done"], 1)
                    act.wait_ge(S["q_in_ps"], b1.n + 1)
                    a.activation(exp_q[:, h, :], q_ps, ACT.Exp, bias=-1.0).then_inc(S["expq_done"], 1)
                if b3 is not None:
                    act.wait_ge(S["turned_in_ps"], b3.n + 1)
                    lo = 0 if b4 is not None else 1
                    a.copy(turned[:, b3.slot(2), lo:2, :], turned_ps[:, lo:2, :]).then_inc(S["turned_done"], 1)
                elif b4 is not None:
                    act.wait_ge(S["turned_in_ps"], b4.n + 2)
                    a.copy(turned[:, (b4.c + 1) % 2, 0, :], turned_ps[:, 0, :]).then_inc(S["turned_done"], 1)
                if b0 is not None:
                    h = b0.slot(2)
                    act.wait_ge(S["nb1_done"], b0.n + 1)
                    for t in range(TB):
                        i = a.activation(xn[:, h, t, :], x_tile(b0, t), ACT.Identity,
                                         bias=nb1[:, h, t:t + 1], scale=rstd1[:, h, t:t + 1])
                    i.then_inc(S["xn_done"], 1)
                if b5 is not None and b5.c % 2 == 1:
                    act.wait_ge(S["gap_done"], pair(b5) + 1)
                    a.activation(exp_gap[:, :], gap[:, :], ACT.Exp).then_inc(S["exp_gap_done"], 1)
                if b3 is not None:
                    h = b3.slot(2)
                    act.wait_ge(S["proj_in_ps"], b3.n + 1)
                    for t in range(TB):
                        i = a.activation(squares[:, h, t, :], proj_ps[:, t, 0, :], ACT.Square,
                                         accum_out=sumsq[:, h, t:t + 1])
                    i.then_inc(S["sumsq_done"], 1)
                if b0 is not None:
                    h = b0.slot(2)
                    for t in range(TB):
                        i = a.activation(xx[:, h, t, :], x_tile(b0, t), ACT.Identity,
                                         bias=nb1[:, h, t:t + 1], scale=rp1[:, h, t:t + 1])
                    i.then_inc(S["xx_done"], 1)
            pass_1(act, step)

            def step(at):
                t3, t5 = at(3), at(5)
                if t5 is not None:
                    h = t5.slot(2)
                    act.wait_ge(S["hid_in_ps"], t5.n + 1)
                    a.activation(hid[:, h, :, :], hid_ps[h], ACT.Gelu).then_inc(S["hid_done"], 1)
                if t3 is not None:
                    h = t3.slot(2)
                    act.wait_ge(S["got_in_ps"], t3.n + 1)
                    a.copy(got_T[:, h, :], got_ps[h]).then_inc(S["got_T_done"], 1)
            pass_2(act, step)

        @block.vector
        def _(dve):
            v = nc.vector
            v.memset(bias3[:, :], 0.0).then_inc(S["bias_step"], 1)
            v.memset(ones_b[:, :], 1.0)
            v.memset(ones_h[:, :], 1.0)
            v.memset(v_sb[:, :, :, D:VW], 1.0)
            dve.wait_ge(S["bias_in"], 48)
            dve.wait_ge(S["bias_step"], 1)
            three = (0, 32, 64)
            for r in three:
                i = v.tensor_scalar_add(bias_f[r:r + 1, 0:2 * D], bias_f[r:r + 1, 0:2 * D], 1.0)
            i.then_inc(S["bias_step"], 1)
            dve.wait_ge(S["bias_step"], 2)

            def split_bias(lo, hi, at_step, name, ready, by):
                v.tensor_copy(bias3[0:1, lo:hi], bias_f[0:1, lo:hi])
                for r in three[1:]:
                    i = v.tensor_copy(bias_h[r:r + 1, lo:hi], bias_f[r:r + 1, lo:hi])
                i.then_inc(S[name], 1)
                dve.wait_ge(S[name], at_step + 1)
                for r in three[1:]:
                    i = v.tensor_tensor(bias_r[r:r + 1, lo:hi], bias_f[r:r + 1, lo:hi], bias_h[r:r + 1, lo:hi],
                                        ALU.subtract)
                i.then_inc(S[name], 1)
                dve.wait_ge(S[name], at_step + 2)
                v.tensor_copy(bias3[32:33, lo:hi], bias_r[32:33, lo:hi])
                v.tensor_copy(bias_m[64:65, lo:hi], bias_r[64:65, lo:hi]).then_inc(S[name], 1)
                dve.wait_ge(S[name], at_step + 3)
                v.tensor_tensor(bias_s[64:65, lo:hi], bias_r[64:65, lo:hi], bias_m[64:65, lo:hi], ALU.subtract)\
                 .then_inc(S[name], 1)
                dve.wait_ge(S[name], at_step + 4)
                v.tensor_copy(bias3[64:65, lo:hi], bias_s[64:65, lo:hi]).then_inc(S[ready], by)
            split_bias(0, 3 * D, 2, "bias_step", "dve_const", 2)

            def prepare_projection():
                dve.wait_ge(S["affine_in"], 32)
                dve.wait_ge(S["weights_in"], 48)
                v.tensor_reduce(wproj_mean[:, :], wproj[:, :], AX.X, ALU.add)
                for r in three:
                    i = v.tensor_reduce(bias_mean[r:r + 1, :], bias_f[r:r + 1, 3 * D:4 * D], AX.X, ALU.add)
                i.then_inc(S["proj_step"], 1)
                dve.wait_ge(S["proj_step"], 1)
                v.tensor_scalar_mul(wproj_mean[:, :], wproj_mean[:, :], 1.0 / D)
                for r in three:
                    i = v.tensor_scalar_mul(bias_mean[r:r + 1, :], bias_mean[r:r + 1, :], 1.0 / D)
                i.then_inc(S["proj_step"], 1)
                dve.wait_ge(S["proj_step"], 2)
                v.tensor_scalar(wproj2[:, 0, :], wproj[:, :], wproj_mean[:, 0:1], None, ALU.subtract)
                v.scalar_tensor_tensor(wproj2[:, 1, :], wproj[:, :], wproj_mean[:, 0:1], gamma_b[:, :],
                                       ALU.subtract, ALU.mult).then_inc(S["proj_const"], 1)
                for r in three:
                    v.scalar_tensor_tensor(bias_f[r:r + 1, 4 * D:5 * D], bias_f[r:r + 1, 3 * D:4 * D],
                                           bias_mean[r:r + 1, 0:1], gamma_b[r:r + 1, :], ALU.subtract, ALU.mult)
                    i = v.tensor_scalar(bias_f[r:r + 1, 3 * D:4 * D], bias_f[r:r + 1, 3 * D:4 * D],
                                        bias_mean[r:r + 1, 0:1], None, ALU.subtract)
                i.then_inc(S["proj_step"], 1)
                dve.wait_ge(S["proj_step"], 3)
                split_bias(3 * D, 5 * D, 3, "proj_step", "proj_const", 1)
                dve.wait_ge(S["router_mean_in_ps"], 1)
                v.tensor_tensor(wr_c[:, :], wr[:, :], wr_mean_ps, ALU.subtract).then_inc(S["router_const"], 1)

            def stats(tag, b, out_stat, src):
                for t in range(TB):
                    i = v.bn_stats(out_stat[:, b.slot(2), t, :], src(t))
                i.then_inc(S[f"stats{tag}_done"], 1)

            def aggregate(tag, b, out_mv, stat):
                dve.wait_ge(S[f"stats{tag}_done"], b.n + 1)
                dve.sem_inc(S["passed_gate"], 1)
                for t in range(TB):
                    i = v.bn_aggr(out_mv(t), stat[:, b.slot(2), t, :])
                i.then_inc(S[f"mv{tag}_done"], 1)

            def per_expert(a):
                return a[:, :].unsqueeze(2).to_broadcast([P, PT, E])

            def step(u, at):
                b0, b1, b2, b3, b4, b5 = at(0), at(1), at(2), at(3), at(4), at(5)
                closes = b5 is not None and b5.c % 2 == 1
                n = pair(b5) if closes else None
                half = (b5.c // 2) % 2 if closes else None
                if closes:
                    dve.wait_ge(S["logits_in_ps"], b5.n + 1)
                    v.tensor_reduce(top1[:, :], logit_ps, AX.X, ALU.max).then_inc(S["top1_done"], 1)
                if b3 is not None:
                    h = b3.slot(2)
                    dve.wait_ge(S["rden_done"], b3.n + 1)
                    v.tensor_tensor(attn[:, h, :, :].rearrange("p d (t g) -> p t g d", t=TB),
                                    num_ps[:, :, 0:D].rearrange("p t (g d) -> p t g d", g=HEADS),
                                    rden[:, h, :, :].unsqueeze(3).to_broadcast([P, TB, HEADS, HD]),
                                    ALU.mult).then_inc(S["attn_done"], 1)
                if closes:
                    dve.wait_ge(S["top1_done"], n + 1)
                    v.tensor_tensor(is_top[:, :, :], logit_ps, per_expert(top1), ALU.is_equal)\
                     .then_inc(S["is_top_done"], 1)
                if b4 is not None:
                    h = b4.slot(2)
                    dve.wait_ge(S["sumsq_done"], b4.n + 1)
                    v.tensor_scalar(var2[:, h, :], sumsq[:, h, :], 1.0 / D, LN_EPS, ALU.mult, ALU.add)\
                     .then_inc(S["var2_done"], 1)
                if b0 is not None:
                    if isinstance(b0.n, int):
                        for c, (lo, _) in enumerate(X_CHUNKS):
                            if b0.n == lo:
                                dve.wait_ge(x_in[c], 16)
                    stats(1, b0, stat1, lambda t: x_tile(b0, t))
                if closes:
                    if b5.least == 1:
                        dve.wait_ge(S["pool_const"], 5)
                    dve.wait_ge(S["is_top_done"], n + 1)
                    v.tensor_tensor(key[:, :, :], is_top[:, :, :], first_key[:, :, :], ALU.mult)\
                     .then_inc(S["key_done"], 1)
                if b3 is not None:
                    h = b3.slot(2)
                    dve.wait_ge(S["attn_done"], b3.n + 1)
                    v.transpose(regrouped[:, h, :, :, :].rearrange("p a d r -> p d a r"),
                                attn[:, h, :, :]).then_inc(S["regrouped_done"], 1)
                if closes:
                    dve.wait_ge(S["key_done"], n + 1)
                    v.tensor_reduce(top_key[:, :], key[:, :, :], AX.X, ALU.max).then_inc(S["top_key_done"], 1)
                if b0 is not None:
                    aggregate(1, b0, lambda t: mv1[:, b0.slot(2), t, :], stat1)
                if b2 is not None:
                    h = b2.slot(2)
                    dve.wait_ge(S["sum_in_ps"], b2.n + 1)
                    v.tensor_tensor(kv_sb[:, h, :], sum_ps, head_mask[:, :], ALU.mult)\
                     .then_inc(S["kvsum_done"], 1)
                if closes:
                    dve.wait_ge(S["top_key_done"], n + 1)
                    v.tensor_tensor(chosen[:, :, :], key[:, :, :], per_expert(top_key), ALU.is_equal)\
                     .then_inc(S["chosen_done"], 1)
                if b0 is not None:
                    h = b0.slot(2)
                    dve.wait_ge(S["mv1_done"], b0.n + 1)
                    v.tensor_scalar_add(var1[:, h, :], mv1[:, h, :, 1], LN_EPS).then_inc(S["var1_done"], 1)
                if b4 is not None:
                    h = b4.slot(2)
                    dve.wait_ge(S["rstd2_done"], b4.n + 1)
                    dve.wait_ge(S["resid_done"], b4.n + 1)
                    if b4.least >= UB:
                        dve.wait_ge(rows_free[b4.slot(UB)], 16 * TB * b4.round())
                    for t in range(TB):
                        i = v.scalar_tensor_tensor(rows[:, b4.slot(UB), t, 0:D], proj_ps[:, t, 1, :],
                                                   rstd2[:, h, t:t + 1], resid[:, b4.slot(UB), t, :],
                                                   ALU.mult, ALU.add)
                    i.then_inc(S["x1_done"], 1)
                if closes:
                    dve.wait_ge(S["chosen_done"], n + 1)
                    v.scalar_tensor_tensor(rest[:, :, :], chosen[:, :, :], NEG_HUGE, logit_ps, ALU.mult, ALU.add)\
                     .then_inc(S["rest_done"], 1)
                if b4 is not None:
                    dve.wait_ge(S["x1_done"], b4.n + 1)
                    stats(3, b4, stat3, lambda t: rows[:, b4.slot(UB), t, 0:D])
                if closes:
                    dve.wait_ge(S["rest_done"], n + 1)
                    v.tensor_reduce(top2[:, :], rest[:, :, :], AX.X, ALU.max).then_inc(S["top2_done"], 1)
                if b0 is not None:
                    h = b0.slot(2)
                    dve.wait_ge(S["rstd1_done"], b0.n + 1)
                    v.scalar_tensor_tensor(nb1[:, h, :], mv1[:, h, :, 0], -1.0, rstd1[:, h, :], ALU.mult, ALU.mult)
                    v.tensor_scalar_add(rp1[:, h, :], rstd1[:, h, :], 1.0).then_inc(S["nb1_done"], 1)
                if b4 is not None:
                    aggregate(3, b4, lambda t: rows[:, b4.slot(UB), t, MEAN:MEAN + 2], stat3)
                if closes:
                    dve.wait_ge(S["top2_done"], n + 1)
                    v.tensor_tensor(diff[:, :], top2[:, :], top1[:, :], ALU.subtract).then_inc(S["diff_done"], 1)
                if b1 is not None:
                    h = b1.slot(2)
                    dve.wait_ge(S["v_done"], b1.n + 1)
                    v.scalar_tensor_tensor(phi_k[:, h, :, :], exp_k[:, h, :, :], 1.0, kv_ps[:, :, 0:D],
                                           ALU.min, ALU.max).then_inc(S["phik_done"], 1)
                if b4 is not None:
                    h = b4.slot(2)
                    dve.wait_ge(S["mv3_done"], b4.n + 1)
                    v.tensor_scalar_add(var3[:, h, :], rows[:, b4.slot(UB), :, RSTD], LN_EPS)\
                     .then_inc(S["var3_done"], 1)
                if closes:
                    dve.wait_ge(S["rstd3_done"], b5.n + 1)
                    dve.wait_ge(S["diff_done"], n + 1)
                    v.tensor_tensor(gap[:, :].rearrange("p (b t) -> p b t", b=2),
                                    diff[:, :].rearrange("p (b t) -> p b t", b=2),
                                    rows[:, 2 * half:2 * half + 2, :, RSTD], ALU.mult).then_inc(S["gap_done"], 1)
                    v.tensor_reduce(n_chosen[:, :], chosen[:, :, :].rearrange("p t e -> p e t"), AX.X, ALU.add)\
                     .then_inc(S["n_chosen_done"], 1)
                if b1 is not None:
                    h = b1.slot(2)
                    dve.wait_ge(S["expq_done"], b1.n + 1)
                    v.scalar_tensor_tensor(phi_q[:, h, :].rearrange("p (c r) -> p r c", r=R),
                                           exp_q[:, h, :].rearrange("p (r c) -> p r c", r=R), 1.0,
                                           q_ps.rearrange("p (r c) -> p r c", r=R), ALU.min, ALU.max)\
                     .then_inc(S["phiq_done"], 1)
                if b0 is not None and b0.least == 1:
                    prepare_projection()
                if closes:
                    dve.wait_ge(S["ranks_in_ps"], n + 1)
                    v.tensor_tensor(pos_sel[:, :, :], rank_ps, chosen[:, :, :], ALU.mult)\
                     .then_inc(S["pos_sel_done"], 1)
                if b2 is not None:
                    h = b2.slot(2)
                    dve.wait_ge(S["num_in_ps"], b2.n + 1)
                    v.tensor_scalar_max(den[:, h, :, :], num_ps[:, :, D:VW], DEN_MIN).then_inc(S["den_done"], 1)
                if closes:
                    dve.wait_ge(S["exp_gap_done"], n + 1)
                    v.tensor_scalar_add(gate_den[:, :], exp_gap[:, :], 1.0).then_inc(S["gate_den_done"], 1)
                    dve.wait_ge(S["n_chosen_done"], n + 1)
                    v.tensor_tensor(seen[:, :], seen[:, :], n_chosen[:, :], ALU.add).then_inc(S["seen_done"], 1)
                if b2 is not None:
                    h = b2.slot(2)
                    dve.wait_ge(S["den_done"], b2.n + 1)
                    v.reciprocal(rden[:, h, :, :], den[:, h, :, :]).then_inc(S["rden_done"], 1)
                if closes:
                    dve.wait_ge(S["gate_den_done"], n + 1)
                    v.reciprocal(rows[:, 2 * half:2 * half + 2, :, GATE],
                                 gate_den[:, :].rearrange("p (b t) -> p b t", b=2))
                    dve.wait_ge(S["pos_sel_done"], n + 1)
                    with nc.allow_low_precision("row numbers are whole and below 2^24"):
                        v.tensor_reduce(pos[:, half, :], pos_sel[:, :, :], AX.X, ALU.add)\
                         .then_inc(S["pos_done"], 1)

            dve.wait_ge(S["pool_const"], 4)
            pass_1(dve, step)

            count = [0]

            def link(ins):
                count[0] += 1
                ins.then_inc(S["table_step"], 1)
                dve.wait_ge(S["table_step"], count[0])
            v.memset(reached[:, :, 0:1], 1.0)
            dve.wait_ge(S["counts_in_ps"], 1)
            link(v.tensor_tensor(n_tok[:, :], count_ps, region_base[:, :], ALU.subtract))
            link(v.tensor_tensor(over[:, :, :], n_tok[:, :].unsqueeze(2).to_broadcast([P, E, TOK // P]),
                                 step_128[:, :, :], ALU.is_gt))
            link(v.tensor_reduce(n_tiles[:, :], over[:, :, :], AX.X, ALU.add))
            link(v.tensor_tensor(tiles_m[:, :, :], n_tiles[:, :].unsqueeze(1).to_broadcast([P, E, E]),
                                 upto[:, :, :], ALU.mult))
            link(v.tensor_reduce(tiles_upto[:, :], tiles_m[:, :, :], AX.X, ALU.add))
            v.tensor_tensor(reached[:, :, 1:E + 1], tile_no[:, :].unsqueeze(2).to_broadcast([P, NT, E]),
                            tiles_upto[:, :].unsqueeze(1).to_broadcast([P, NT, E]), ALU.is_ge)
            link(v.tensor_tensor(tiles_before[:, :], tiles_upto[:, :], n_tiles[:, :], ALU.subtract))
            v.tensor_tensor(mine[:, :, :], reached[:, :, 0:E], reached[:, :, 1:E + 1], ALU.subtract)
            link(v.scalar_tensor_tensor(row_base[:, :], tiles_before[:, :], float(P), count_ps, ALU.mult, ALU.add))
            link(v.tensor_tensor(row_of[:, :, :], row_base[:, :].unsqueeze(1).to_broadcast([P, NT, E]),
                                 tile_end[:, :].unsqueeze(2).to_broadcast([P, NT, E]), ALU.subtract))
            v.tensor_reduce(passed[:, :], reached[:, :, 1:E + 1], AX.X, ALU.add)
            link(v.tensor_tensor(row_sel[:, :, :], row_of[:, :, :], mine[:, :, :], ALU.mult))
            v.tensor_scalar_min(tile_expert[:, :], passed[:, :], float(E - 1))
            with nc.allow_low_precision("row numbers are whole and below 2^24"):
                v.tensor_reduce(tile_row[:, :], row_sel[:, :, :], AX.X, ALU.add).then_inc(S["table_done"], 1)
            dve.wait_ge(S["table_done"], 1)
            dve.wait_ge(S["ffn_in"], 32)

            def step(at):
                t2, t3, t5 = at(2), at(3), at(5)
                if t3 is not None:
                    h = t3.slot(2)
                    expert = dve.value_load(tile_expert[0:1, bass.ds(t3.n, 1)], min_val=0, max_val=E - 1)
                    if t3.least >= 2:
                        dve.wait_ge(S["hid_in_ps"], t3.n - 1)
                    v.tensor_copy(w1_tile[:, h, :], w1_sb[:, bass.ds(expert * HID, HID)])\
                     .then_inc(S["w1_tile_done"], 1)
                if t2 is not None:
                    h = t2.slot(2)
                    s = t2.slot(UT)
                    dve.wait_ge(got_in[s], 16 * (t2.round() + 1))
                    if t2.least >= 2:
                        dve.wait_ge(S["got_in_ps"], t2.n - 1)
                    v.tensor_scalar(got_n[:, h, :], got[:, s, 0:D], got[:, s, MEAN:MEAN + 1],
                                    got[:, s, RSTD:RSTD + 1], ALU.subtract, ALU.mult).then_inc(S["got_n_done"], 1)
                if t5 is not None:
                    h = t5.slot(2)
                    s = t5.slot(UT)
                    dve.wait_ge(S["y_in_ps"], t5.n + 1)
                    if t5.least >= UT:
                        dve.wait_ge(out_done[s], 16 * t5.round())
                    v.tensor_copy(done_token[:, s:s + 1], got[:, s, TOKEN:TOKEN + 1].bitcast(I32))
                    v.scalar_tensor_tensor(done[:, s, :], y_ps[h], got[:, s, GATE:GATE + 1], got[:, s, 0:D],
                                           ALU.mult, ALU.add).then_inc(S["done_ready"], 1)
            pass_2(dve, step)


def kernel(L0_attn_H, L0_attn_W_qkv, L0_attn_b_qkv, L0_attn_W_proj, L0_attn_b_proj, L0_attn_gamma,
           L0_attn_beta, L0_ffn_Wr, L0_ffn_W1, L0_ffn_W2):
    import numpy as np
    import concourse.bacc as bacc
    from concourse.bass_utils import run_bass_kernel_spmd as run

    H = np.asarray(L0_attn_H)
    B, N, D = H.shape
    W1, W2 = np.asarray(L0_ffn_W1), np.asarray(L0_ffn_W2)
    E, _, HID = W1.shape
    bias = np.concatenate([np.asarray(L0_attn_b_qkv), np.asarray(L0_attn_b_proj)])
    split = (B, 16, 2, 4, 2, D)
    x = H.reshape(split).transpose(3, 2, 1, 0, 4, 5).reshape(128, B, 2 * D)
    wproj_t = np.asarray(L0_attn_W_proj).T.reshape(2, 4, 2, 8, D).transpose(3, 2, 1, 0, 4).reshape(D, D)
    arrays = {
        "x": x,
        "wqkv_t": np.asarray(L0_attn_W_qkv).T,
        "b_all": np.broadcast_to(bias, (3, bias.size)),
        "wproj_t": wproj_t,
        "gamma": np.asarray(L0_attn_gamma),
        "beta": np.asarray(L0_attn_beta),
        "w_router": np.asarray(L0_ffn_Wr),
        "w1": W1.transpose(1, 0, 2).reshape(D, E * HID),
        "w2": W2.reshape(E, HID // 128, 128, D).transpose(2, 0, 1, 3).reshape(128, E * HID),
    }
    arrays = {k: np.ascontiguousarray(a) for k, a in arrays.items()}
    nc = bacc.Bacc("TRN2", target_bir_lowering=False, num_devices=1)
    args = [nc.dram_tensor(k, a.shape, F32, kind="ExternalInput").ap() for k, a in arrays.items()]
    args.append(nc.dram_tensor("out", [B * N, D], F32, kind="ExternalOutput").ap())
    build(nc, *args)
    r = run(nc, [arrays], core_ids=[0])
    return r.results[0]["out"].reshape(B, 4, 2, 16, 2, D).transpose(0, 3, 2, 1, 4, 5).reshape(H.shape)
```

```python
from contextlib import ExitStack

import concourse.bass as bass
from concourse import mybir

ALU = mybir.AluOpType
ACT = mybir.ActivationFunctionType
AX = mybir.AxisListType
F32 = mybir.dt.float32
F16 = mybir.dt.float16
BF16 = mybir.dt.bfloat16
I32 = mybir.dt.int32

P = 128
LN_EPS = 1e-5
DEN_MIN = 1e-6
NEG_HUGE = -3.0e38


class Item:

    def __init__(self, unroll, j, c, j_min=0):
        self.unroll, self.j, self.c = unroll, j, c
        self.n = unroll * j + c
        self.least = unroll * (j if isinstance(j, int) else j_min) + c

    def slot(self, k):
        return self.c % k

    def round(self):
        return self.j + self.c // self.unroll

    def least_round(self):
        return self.least // self.unroll


def build(nc, x, wqkv_t, b_all, wproj_t, gamma, beta, w_router, w1, w2, out):
    D = wproj_t.shape[0]
    TOK = x.shape[0] * x.shape[1] * x.shape[2] // D
    E = w_router.shape[1]
    HID = w1.shape[1] // E
    HEADS = 16
    HD = D // HEADS
    CH = HID // P
    TB = 2
    SEQ = TB * P
    NB = TOK // SEQ
    VW = D + HEADS
    UB = 4
    PT = 2 * TB
    REGION = TOK + P
    ROW = D + 4
    MEAN, RSTD, GATE, TOKEN = D, D + 1, D + 2, D + 3
    NT = TOK // P + E - 1
    UT = 6
    LAG_B, LAG_T = 8, 5
    assert D == P and NB % UB == 0 and HID % P == 0

    R = SEQ // HEADS
    assert R == HEADS == 16
    rows_dram = nc.dram_tensor("expert_rows", [E * REGION, ROW], F32, kind="Internal").ap()

    with ExitStack() as ctx:
        def sb(name, shape, dt=F32):
            return ctx.enter_context(nc.sbuf_tensor(name, shape, dt))

        def ps(name, shape):
            return ctx.enter_context(nc.psum_tensor(name, shape, F32))

        def sem(name):
            return ctx.enter_context(nc.semaphore(name))

        wqkv = sb("wqkv", [P, 3 * D])
        wproj = sb("wproj", [P, D])
        wproj_mean = sb("wproj_mean", [P, 1])
        wproj2 = sb("wproj2", [P, 2, D])
        wr = sb("wr", [P, E])
        wr_c = sb("wr_c", [P, E])
        w1_sb = sb("w1_sb", [P, E * HID])
        w2_sb = sb("w2_sb", [P, E * HID])
        gamma_b = sb("gamma_b", [P, D])
        beta_b = sb("beta_b", [P, D])
        bias_f = sb("bias_f", [P, 5 * D])
        bias_mean = sb("bias_mean", [P, 1])
        bias_r = sb("bias_r", [P, 5 * D])
        bias_s = sb("bias_s", [P, 5 * D])
        bias3 = sb("bias3", [P, 5 * D], BF16)
        bias_h = sb("bias_h", [P, 5 * D], BF16)
        bias_m = sb("bias_m", [P, 5 * D], BF16)
        ones_b = sb("ones_b", [P, 4 * P], BF16)
        ones_h = sb("ones_h", [P, P], F16)
        before = sb("before", [P, P], F16)
        ident = sb("ident", [P, P])
        averaging = sb("averaging", [P, P])
        head_mask = sb("head_mask", [P, VW])
        neg_half = sb("neg_half", [P, 3, TB])
        first_key = sb("first_key", [P, PT, E])
        token_no = sb("token_no", [P, NB * TB], I32)
        region_base = sb("region_base", [P, E])
        step_128 = sb("step_128", [P, E, TOK // P])
        upto = sb("upto", [P, E, E])
        tile_no = sb("tile_no", [P, NT])
        tile_end = sb("tile_end", [P, NT])
        pad_rows = sb("pad_rows", [P, ROW])

        x_sb = sb("x_sb", [P, NB, SEQ])
        stat1 = sb("stat1", [P, 2, TB, 6])
        moments = sb("moments", [P, 2, 3, TB, 2])
        nb1 = sb("nb1", [P, 2, TB])
        rp1 = sb("rp1", [P, 2, TB])
        xn = sb("xn", [P, 2, TB, D])
        xx = sb("xx", [P, 2, TB, D])
        resid = sb("resid", [P, UB, TB, D])
        xnT = sb("xnT", [P, 2, SEQ])
        exp_q = sb("exp_q", [P, 2, SEQ])
        exp_k = sb("exp_k", [P, 2, TB, D])
        phi_q = sb("phi_q", [P, 2, SEQ])
        phi_k = sb("phi_k", [P, 2, TB, D])
        v_sb = sb("v_sb", [P, 2, TB, VW])
        kv_sb = sb("kv_sb", [P, 2, VW])
        den = sb("den", [P, 2, TB, HEADS])
        rden = sb("rden", [P, 2, TB, HEADS])
        attn = sb("attn", [P, 2, HD, 2 * HEADS])
        regrouped = sb("regrouped", [P, 2, TB, HD, R])
        attnT = sb("attnT", [P, 2, SEQ])
        x1T = sb("x1T", [P, 2, SEQ])
        squares = sb("squares", [P, 2, TB, D], BF16)
        rows = sb("rows", [P, UB, TB, ROW])
        stat3 = sb("stat3", [P, 2, TB, 6])
        logits = sb("logits", [P, PT, E])
        top1 = sb("top1", [P, PT])
        is_top = sb("is_top", [P, PT, E])
        key = sb("key", [P, PT, E])
        top_key = sb("top_key", [P, PT])
        chosen = sb("chosen", [P, PT, E], F16)
        rest = sb("rest", [P, PT, E])
        top2 = sb("top2", [P, PT])
        diff = sb("diff", [P, PT])
        gap = sb("gap", [P, PT])
        exp_gap = sb("exp_gap", [P, PT])
        gate_den = sb("gate_den", [P, PT])
        n_chosen = sb("n_chosen", [P, E])
        seen = sb("seen", [P, E], F16)
        pos_sel = sb("pos_sel", [P, PT, E])
        pos = sb("pos", [P, 2, PT], I32)
        n_tok = sb("n_tok", [P, E])
        over = sb("over", [P, E, TOK // P])
        n_tiles = sb("n_tiles", [P, E])
        tiles_m = sb("tiles_m", [P, E, E])
        tiles_upto = sb("tiles_upto", [P, E])
        tiles_before = sb("tiles_before", [P, E])
        row_base = sb("row_base", [P, E])
        reached = sb("reached", [P, NT, E + 1])
        mine = sb("mine", [P, NT, E])
        row_of = sb("row_of", [P, NT, E])
        row_sel = sb("row_sel", [P, NT, E])
        passed = sb("passed", [P, NT])
        tile_row = sb("tile_row", [P, NT], I32)
        tile_expert = sb("tile_expert", [P, NT], I32)

        got = sb("got", [P, UT, ROW])
        got_n = sb("got_n", [P, 2, D])
        got_T = sb("got_T", [P, 2, P])
        w1_tile = sb("w1_tile", [P, 2, HID])
        hid = sb("hid", [P, 2, CH, P])
        done = sb("done", [P, UT, D])
        done_token = sb("done_token", [P, UT], I32)

        bank = [ps(f"bank{i}", [P, 512]) for i in range(8)]
        xnT_ps = bank[0][:, 0:SEQ]
        attnT_ps = bank[1][:, 0:SEQ]
        x1T_ps = bank[1][:, SEQ:2 * SEQ]
        sum_ps = bank[2][:, 0:VW]
        q_ps = bank[3][:, 0:SEQ]
        kv_ps = bank[4][:, :].rearrange("p (t c) -> p t c", t=TB)
        num_ps = bank[5][:, 0:TB * VW].rearrange("p (t c) -> p t c", t=TB)
        proj_ps = [bank[6 + h][:, :].rearrange("p (t k c) -> p t k c", t=TB, k=2) for h in range(2)]
        logit_ps = bank[2][:, 256:256 + PT * E].rearrange("p (t e) -> p t e", t=PT)
        rank_ps = bank[2][:, 320:320 + PT * E].rearrange("p (t e) -> p t e", t=PT)
        count_ps = bank[2][:, 384:384 + E]
        wr_mean_ps = bank[7][:, 0:E]
        got_ps = [bank[0 + h][:, 0:P] for h in range(2)]
        hid_ps = [bank[2 + h][:, :].rearrange("p (c t) -> p c t", c=CH) for h in range(2)]
        y_ps = [bank[4 + h][:, 0:D] for h in range(2)]

        S = {n: sem(n) for n in (
            "weights_in", "bias_in", "affine_in", "ffn_in",
            "pool_const", "ones_ready", "dve_const", "bias_step", "proj_step", "proj_const",
            "router_mean_in_ps",
            "router_const", "mask_step",
            "stats1_done", "moments1_done", "moments3_done", "eps_added", "rstd_done", "nb1_done",
            "xn_done", "xx_done", "resid_done", "xnT_in_ps", "xnT_done", "q_in_ps", "kv_in_ps",
            "expk_done", "v_done", "expq_done", "phik_done", "phiq_done", "sum_in_ps",
            "kvsum_done", "num_in_ps", "den_done", "rden_done", "attn_done", "regrouped_done",
            "attnT_in_ps", "attnT_done", "proj_in_ps", "moments2_done", "x1_done", "x1T_in_ps",
            "x1T_done", "stats3_done", "row_tail_done",
            "logits_in_ps", "logits_read", "top1_done", "is_top_done", "key_done",
            "top_key_done", "chosen_done", "rest_done", "top2_done", "diff_done", "gap_done",
            "exp_gap_done", "gate_den_done", "n_chosen_done", "ranks_in_ps", "pos_sel_done",
            "seen_done", "pos_done", "counts_in_ps", "table_step", "table_done",
            "got_n_done", "got_in_ps", "got_T_done", "w1_tile_done", "hid_in_ps", "hid_done",
            "y_in_ps", "done_ready", "passed_gate")}
        x_in = [sem(f"x_in{c}") for c in range(4)]
        rows_free = [sem(f"rows_free{h}") for h in range(UB)]
        got_in = [sem(f"got_in{h}") for h in range(UT)]
        out_done = [sem(f"out_done{h}") for h in range(UT)]

        BUSY_AT_START, BUSY_AT_END, BUSY_BETWEEN = 12, 8, 11
        X_CHUNKS = [(0, 1), (1, 2), (2, 4), (4, NB)]

        def pass_1(eng, step):
            def peeled(s):
                def at(lag):
                    return Item(UB, (s - lag) // UB, (s - lag) % UB) if 0 <= s - lag < NB else None
                step(s, at)
            first = 2 * UB
            for s in range(first):
                peeled(s)
            with eng.Fori(first // UB, NB // UB) as j:
                for u in range(UB):
                    step(u, lambda lag: Item(UB, j, u - lag, first // UB))
            for s in range(NB, NB + LAG_B):
                peeled(s)

        def pass_2(eng, step):
            def peeled(s):
                def at(lag):
                    return Item(UT, (s - lag) // UT, (s - lag) % UT) if 0 <= s - lag < NT else None
                step(at)
            first = 2 * UT
            for s in range(first):
                peeled(s)
            with eng.Fori(first // UT, NT // UT) as j:
                for u in range(UT):
                    step(lambda lag: Item(UT, j, u - lag, first // UT))
            for s in range(NT // UT * UT, NT + LAG_T):
                peeled(s)

        def pair(b):
            return UB // 2 * b.j + b.c // 2

        def span(b1, b5, b6):
            there = [k for k, b in enumerate((b1, b5, b6)) if b is not None]
            return (there[0], there[-1] + 1) if there else (0, 0)

        def rounds_of_std(b1, b5, b6):
            return next(b.n + lag for b, lag in ((b1, 1), (b5, 5), (b6, 6)) if b is not None)

        def x_tile(b, t):
            return x_sb[:, bass.ds(b.n, 1), t * D:t * D + D].rearrange("p a d -> p (a d)")

        block = ctx.enter_context(nc.Block())

        @block.sync
        def _(sp):
            def load_x(c):
                lo, hi = X_CHUNKS[c]
                sp.dma_start(x_sb[:, lo:hi, :], x[:, lo:hi, :]).then_inc(x_in[c], 16)
            load_x(0)
            sp.dma_start(wqkv[:, :], wqkv_t).then_inc(S["weights_in"], 16)
            load_x(1)
            load_x(2)
            sp.dma_start(wproj[:, :], wproj_t).then_inc(S["weights_in"], 16)
            sp.dma_start(wr[:, :], w_router).then_inc(S["weights_in"], 16)
            load_x(3)
            sp.dma_start(w1_sb[:, :], w1).then_inc(S["ffn_in"], 16)
            sp.dma_start(w2_sb[:, :], w2).then_inc(S["ffn_in"], 16)
            sp.wait_ge(S["table_done"], 1)
            for h in range(UB):
                sp.wait_ge(rows_free[h], 16 * (1 + TB * (NB // UB)))

            def step(at):
                t = at(0)
                if t is not None:
                    row = sp.value_load(tile_row[0:1, bass.ds(t.n, 1)], min_val=0, max_val=E * REGION - P)
                    if t.least >= UT:
                        sp.wait_ge(S["done_ready"], t.n - UT + 1)
                    sp.dma_start(got[:, t.slot(UT), :], rows_dram[bass.ds(row, P), :])\
                      .then_inc(got_in[t.slot(UT)], 16)
            pass_2(sp, step)
            for h in range(UT):
                sp.wait_ge(out_done[h], 16 * ((NT - 1 - h) // UT + 1))

        @block.gpsimd
        def _(pool):
            g = nc.gpsimd
            g.memset(pad_rows[:, :], 0.0).then_inc(S["mask_step"], 1)
            pool.wait_ge(S["mask_step"], 1)
            g.iota(pad_rows[:, TOKEN:TOKEN + 1].bitcast(I32), pattern=[[1, 1]], base=TOK,
                   channel_multiplier=1).then_inc(S["pool_const"], 1)
            g.memset(neg_half[:, :], -0.5)
            g.memset(averaging[:, :], 1.0 / P)
            g.memset(ident[:, :], 0.0).then_inc(S["mask_step"], 1)
            pool.wait_ge(S["mask_step"], 2)
            g.affine_select(out=ident[:, :], in_=ident[:, :], compare_op=ALU.not_equal, fill=1.0,
                            base=0, pattern=[[-1, P]], channel_multiplier=1).then_inc(S["pool_const"], 1)
            g.memset(head_mask[:, :], 1.0).then_inc(S["mask_step"], 1)
            pool.wait_ge(S["mask_step"], 3)
            parts = [(head_mask[:, 0:D], [[-HD, HEADS], [0, HD]]), (head_mask[:, D:VW], [[-HD, HEADS]])]
            for m, pat in parts:
                g.affine_select(out=m, in_=m, compare_op=ALU.is_ge, fill=0.0, base=0, pattern=pat,
                                channel_multiplier=1).then_inc(S["mask_step"], 1)
            pool.wait_ge(S["mask_step"], 5)
            for m, pat in parts:
                g.affine_select(out=m, in_=m, compare_op=ALU.is_ge, fill=0.0, base=HD - 1,
                                pattern=[[-a, n] for a, n in pat], channel_multiplier=-1)\
                 .then_inc(S["pool_const"], 1)

            def more_constants():
                g.memset(before[:, :], 1.0).then_inc(S["mask_step"], 1)
                g.memset(upto[:, :, :], 1.0).then_inc(S["mask_step"], 1)
                pool.wait_ge(S["mask_step"], 7)
                g.affine_select(out=before[:, :], in_=before[:, :], compare_op=ALU.is_gt, fill=0.0, base=0,
                                pattern=[[1, P]], channel_multiplier=-1)
                g.affine_select(out=upto[:, :, :], in_=upto[:, :, :], compare_op=ALU.is_ge, fill=0.0,
                                base=0, pattern=[[1, E], [-1, E]], channel_multiplier=0)
                g.iota(first_key[:, :, :], pattern=[[0, PT], [-1, E]], base=E, channel_multiplier=0,
                       allow_small_or_imprecise_dtypes=True)
                g.iota(seen[:, :], pattern=[[REGION // P, E]], base=1, channel_multiplier=0,
                       allow_small_or_imprecise_dtypes=True)
                g.iota(token_no[:, :].rearrange("p (b t) -> p b t", t=TB), pattern=[[SEQ, NB], [1, TB]],
                       base=0, channel_multiplier=TB)
                g.iota(region_base[:, :], pattern=[[REGION, E]], base=P, channel_multiplier=0,
                       allow_small_or_imprecise_dtypes=True)
                g.iota(step_128[:, :, :], pattern=[[0, E], [P, TOK // P]], base=0, channel_multiplier=0,
                       allow_small_or_imprecise_dtypes=True)
                g.iota(tile_no[:, :], pattern=[[1, NT]], base=0, channel_multiplier=0,
                       allow_small_or_imprecise_dtypes=True)
                g.iota(tile_end[:, :], pattern=[[P, NT]], base=P, channel_multiplier=0,
                       allow_small_or_imprecise_dtypes=True).then_inc(S["pool_const"], 1)

            def write_padding(h):
                each = E // UB
                g.dma_start(rows_dram.rearrange("(e r) c -> r e c", e=E)[0:P, each * h:each * (h + 1)],
                            pad_rows[:, :].unsqueeze(1).to_broadcast([P, each, ROW]))\
                 .then_inc(rows_free[h], 16)

            def scatter(b, last, tile):
                g.indirect_dma_start(
                    out=rows_dram, in_=rows[:, (b.c - (not last)) % UB, tile, :],
                    out_offset=bass.IndirectOffsetOnAxis(
                        ap=pos[:, (b.c // 2) % 2, TB * last + tile:TB * last + tile + 1], axis=0),
                    in_offset=None, bounds_check=E * REGION - 1, oob_is_err=False)\
                 .then_inc(rows_free[(b.c - (not last)) % UB], 16)

            def scatter_going(b7, b8, tiles):
                going = next(((b, last) for b, last in ((b7, 0), (b8, 1))
                              if b is not None and b.c % 2 == 1), None)
                if going:
                    if not going[1] and tiles[0] == 0:
                        pool.wait_ge(S["pos_done"], pair(b7) + 1)
                        pool.wait_ge(S["row_tail_done"], b7.n + 1)
                        pool.sem_inc(S["passed_gate"], 1)
                    for t in tiles:
                        scatter(*going, t)

            def step(u, at):
                b1, b2, b5, b6, b7, b8 = at(1), at(2), at(5), at(6), at(7), at(8)
                if b5 is None:
                    scatter_going(b7, b8, (0,))
                lo, hi = span(b1, b5, b6)
                if lo < hi:
                    pool.wait_ge(S["eps_added"], rounds_of_std(b1, b5, b6))
                    w = moments[:, u % 2, lo:hi, :, 1]
                    g.tensor_tensor(w, w, neg_half[:, lo:hi, :], ALU.pow).then_inc(S["rstd_done"], 1)
                if b1 is not None and b1.least < UB:
                    write_padding(b1.least)
                if b1 is not None and b1.least == UB:
                    more_constants()
                if b6 is not None:
                    if b6.least == 0:
                        pool.wait_ge(S["pool_const"], 5)
                    g.tensor_copy(rows[:, b6.slot(UB), :, TOKEN].bitcast(I32),
                                  token_no[:, bass.ds(TB * b6.n, TB)])
                    pool.wait_ge(S["rstd_done"], rounds_of_std(b1, b5, b6))
                    pool.sem_inc(S["passed_gate"], 1)
                    g.tensor_copy(rows[:, b6.slot(UB), :, MEAN:MEAN + 2], moments[:, u % 2, 2, :, :])\
                     .then_inc(S["row_tail_done"], 1)
                scatter_going(b7, b8, (0, 1) if b5 is not None else (1,))
                if b2 is not None:
                    h = b2.slot(2)
                    if b2.least == 0:
                        pool.wait_ge(S["affine_in"], 32)
                    pool.wait_ge(S["xx_done"], b2.n + 1)
                    g.tensor_tensor(resid[:, b2.slot(UB), :, :], xx[:, h, :, :],
                                    beta_b[:, :].unsqueeze(1).to_broadcast([P, TB, D]), ALU.add)\
                     .then_inc(S["resid_done"], 1)
            pass_1(pool, step)

            def step(at):
                t = at(5)
                if t is not None:
                    pool.wait_ge(S["done_ready"], t.n + 1)
                    pool.sem_inc(S["passed_gate"], 1)
                    g.indirect_dma_start(
                        out=out, out_offset=bass.IndirectOffsetOnAxis(
                            ap=done_token[:, t.slot(UT):t.slot(UT) + 1], axis=0),
                        in_=done[:, t.slot(UT), :], in_offset=None, bounds_check=TOK - 1, oob_is_err=False)\
                     .then_inc(out_done[t.slot(UT)], 16)
            pass_2(pool, step)

        @block.tensor
        def _(pe):
            t_ = nc.tensor

            def keep_busy(n, out):
                for _ in range(n):
                    t_.matmul(out, ones_b[:, 0:P], ones_b[:, :], start=True, stop=True)

            pe.wait_ge(S["ones_ready"], 1)
            keep_busy(BUSY_AT_START, bank[5][:, :])
            pe.wait_ge(S["pool_const"], 2)

            def step(u, at):
                b1, b2, b3, b4, b5, b6 = at(1), at(2), at(3), at(4), at(5), at(6)
                closes = b6 is not None and b6.c % 2 == 1
                n = pair(b6) if closes else None
                if b3 is not None:
                    h = b3.slot(2)
                    pe.wait_ge(S["phik_done"], b3.n + 1)
                    pe.wait_ge(S["v_done"], b3.n + 1)
                    if closes:
                        pe.wait_ge(S["logits_read"], n + 1)
                    for t in range(TB):
                        mm = t_.matmul(sum_ps, phi_k[:, h, t, :], v_sb[:, h, t, :],
                                       start=t == 0, stop=t == TB - 1)
                    mm.then_inc(S["sum_in_ps"], 1)
                if b2 is not None:
                    h = b2.slot(2)
                    if b2.least == 0:
                        pe.wait_ge(S["weights_in"], 16)
                        pe.wait_ge(S["dve_const"], 2)
                    pe.wait_ge(S["xnT_done"], b2.n + 1)
                    for t in range(TB):
                        t_.matmul(kv_ps[:, t, :], ones_b[:, 0:P], bias3[:, D:3 * D], start=True, stop=False)
                        mm = t_.matmul(kv_ps[:, t, :], xnT[:, h, P * t:P * t + P], wqkv[:, D:3 * D],
                                       start=False, stop=True)
                    mm.then_inc(S["kv_in_ps"], 1)
                if b4 is not None:
                    h = b4.slot(2)
                    pe.wait_ge(S["regrouped_done"], b4.n + 1)
                    for t in range(TB):
                        mm = t_.transpose(attnT_ps[:, P * t:P * t + P],
                                          regrouped[:, h, t, :, :].rearrange("p d r -> p (d r)"), ident[:, :])
                    mm.then_inc(S["attnT_in_ps"], 1)
                if b3 is not None:
                    h = b3.slot(2)
                    pe.wait_ge(S["kvsum_done"], b3.n + 1)
                    pe.wait_ge(S["phiq_done"], b3.n + 1)
                    for t in range(TB):
                        mm = t_.matmul(num_ps[:, t, :], phi_q[:, h, P * t:P * t + P], kv_sb[:, h, :],
                                       start=True, stop=True)
                    mm.then_inc(S["num_in_ps"], 1)
                if b2 is not None:
                    h = b2.slot(2)
                    if b2.least >= 1:
                        pe.wait_ge(S["phiq_done"], b2.n)
                    t_.matmul(q_ps, bias3[:, 0:D], ones_b[:, 0:SEQ], start=True, stop=False)
                    t_.matmul(q_ps, wqkv[:, 0:D], xnT[:, h, :], start=False, stop=True)\
                      .then_inc(S["q_in_ps"], 1)
                if b4 is None and b5 is not None:
                    keep_busy(BUSY_AT_END, bank[5][:, :])
                if b5 is not None:
                    pe.wait_ge(S["x1_done"], b5.n + 1)
                    if b4 is not None:
                        pe.wait_ge(S["attnT_done"], b4.n + 1)
                    for t in range(TB):
                        mm = t_.transpose(x1T_ps[:, P * t:P * t + P], rows[:, b5.slot(UB), t, 0:D], ident[:, :])
                    mm.then_inc(S["x1T_in_ps"], 1)
                if closes:
                    if b6.least == 1:
                        pe.wait_ge(S["pool_const"], 5)
                    pe.wait_ge(S["chosen_done"], n + 1)
                    if b6.least >= 2:
                        pe.wait_ge(S["seen_done"], n)
                    t_.matmul(rank_ps, ones_h[:, :], seen[:, :].unsqueeze(1).to_broadcast([P, PT, E]),
                              start=True, stop=False)
                    for t in range(PT - 1):
                        t_.matmul(rank_ps[:, t + 1:PT, :], ones_h[:, :],
                                  chosen[:, t:t + 1, :].to_broadcast([P, PT - 1 - t, E]),
                                  start=False, stop=False)
                    t_.matmul(rank_ps, before[:, :], chosen[:, :, :], start=False, stop=True)\
                      .then_inc(S["ranks_in_ps"], 1)
                if b4 is not None:
                    h = b4.slot(2)
                    pe.wait_ge(S["attnT_done"], b4.n + 1)
                    if b4.least == 0:
                        pe.wait_ge(S["proj_const"], 2)
                        pe.wait_ge(S["router_const"], 1)
                    for t in range(TB):
                        t_.matmul(proj_ps[h][:, t, :, :], ones_b[:, 0:P], bias3[:, 3 * D:5 * D],
                                  start=True, stop=False)
                        mm = t_.matmul(proj_ps[h][:, t, :, :], attnT[:, h, P * t:P * t + P], wproj2[:, :, :],
                                       start=False, stop=True)
                    mm.then_inc(S["proj_in_ps"], 1)
                if b5 is not None:
                    h = b5.slot(2)
                    pe.wait_ge(S["x1T_done"], b5.n + 1)
                    if closes:
                        pe.wait_ge(S["pos_sel_done"], n + 1)
                    for t in range(TB):
                        mm = t_.matmul(logit_ps[:, TB * h + t, :], x1T[:, h, P * t:P * t + P], wr_c[:, :],
                                       start=True, stop=True)
                    mm.then_inc(S["logits_in_ps"], 1)
                if b1 is not None:
                    h = b1.slot(2)
                    pe.wait_ge(S["xn_done"], b1.n + 1)
                    for t in range(TB):
                        mm = t_.transpose(xnT_ps[:, P * t:P * t + P], xn[:, h, t, :], ident[:, :])
                    mm.then_inc(S["xnT_in_ps"], 1)
                    if b1.least == 0:
                        pe.wait_ge(S["weights_in"], 48)
                        t_.matmul(wr_mean_ps, averaging[:, :], wr[:, :], start=True, stop=True)\
                          .then_inc(S["router_mean_in_ps"], 1)

            pass_1(pe, step)
            pe.wait_ge(S["seen_done"], NB // 2)
            pe.wait_ge(S["pos_sel_done"], NB // 2)
            t_.matmul(count_ps, ones_h[:, :], seen[:, :], start=True, stop=True).then_inc(S["counts_in_ps"], 1)

            pe.wait_ge(S["ffn_in"], 32)
            pe.wait_ge(S["table_done"], 1)
            keep_busy(BUSY_BETWEEN, bank[7][:, :])

            def step(at):
                t3, t4, t5 = at(3), at(4), at(5)
                if t3 is not None:
                    h = t3.slot(2)
                    pe.wait_ge(S["got_n_done"], t3.n + 1)
                    t_.transpose(got_ps[h], got_n[:, h, :], ident[:, :]).then_inc(S["got_in_ps"], 1)
                if t4 is not None:
                    h = t4.slot(2)
                    pe.wait_ge(S["got_T_done"], t4.n + 1)
                    pe.wait_ge(S["w1_tile_done"], t4.n + 1)
                    for c in range(CH):
                        mm = t_.matmul(hid_ps[h][:, c, :], w1_tile[:, h, P * c:P * c + P], got_T[:, h, :],
                                       start=True, stop=True)
                    mm.then_inc(S["hid_in_ps"], 1)
                if t5 is not None:
                    h = t5.slot(2)
                    expert = pe.value_load(tile_expert[0:1, bass.ds(t5.n, 1)], min_val=0, max_val=E - 1)
                    pe.wait_ge(S["hid_done"], t5.n + 1)
                    if t5.least >= 2:
                        pe.wait_ge(S["done_ready"], t5.n - 1)
                    for c in range(CH):
                        mm = t_.matmul(y_ps[h], hid[:, h, c, :], w2_sb[:, bass.ds(expert * HID + P * c, P)],
                                       start=c == 0, stop=c == CH - 1)
                    mm.then_inc(S["y_in_ps"], 1)
            pass_2(pe, step)

        @block.scalar
        def _(act):
            a = nc.scalar
            act.dma_start(bias_f[0:65, 0:4 * D], b_all.partition_broadcast(65)).then_inc(S["bias_in"], 16)
            act.dma_start(gamma_b[:, :], gamma.partition_broadcast(P)).then_inc(S["affine_in"], 16)
            act.dma_start(beta_b[:, :], beta.partition_broadcast(P)).then_inc(S["affine_in"], 16)

            def step(u, at):
                b1, b2, b4, b5, b6 = at(1), at(2), at(4), at(5), at(6)
                if b2 is not None:
                    h = b2.slot(2)
                    for t in range(TB):
                        i = a.activation(xx[:, h, t, :], x_tile(b2, t), ACT.Identity,
                                         bias=nb1[:, h, t:t + 1], scale=rp1[:, h, t:t + 1])
                    i.then_inc(S["xx_done"], 1)
                if b2 is not None:
                    h = b2.slot(2)
                    act.wait_ge(S["kv_in_ps"], b2.n + 1)
                    a.copy(v_sb[:, h, :, 0:D], kv_ps[:, :, D:2 * D]).then_inc(S["v_done"], 1)
                    a.activation(exp_k[:, h, :, :], kv_ps[:, :, 0:D], ACT.Exp, bias=-1.0).then_inc(S["expk_done"], 1)
                if b4 is not None:
                    act.wait_ge(S["attnT_in_ps"], b4.n + 1)
                    a.copy(attnT[:, b4.slot(2), :], attnT_ps).then_inc(S["attnT_done"], 1)
                if b2 is not None:
                    h = b2.slot(2)
                    act.wait_ge(S["q_in_ps"], b2.n + 1)
                    a.activation(exp_q[:, h, :], q_ps, ACT.Exp, bias=-1.0).then_inc(S["expq_done"], 1)
                if b5 is not None:
                    act.wait_ge(S["x1T_in_ps"], b5.n + 1)
                    a.copy(x1T[:, b5.slot(2), :], x1T_ps).then_inc(S["x1T_done"], 1)
                if b1 is not None:
                    h = b1.slot(2)
                    act.wait_ge(S["nb1_done"], b1.n + 1)
                    for t in range(TB):
                        i = a.activation(xn[:, h, t, :], x_tile(b1, t), ACT.Identity,
                                         bias=nb1[:, h, t:t + 1], scale=moments[:, u % 2, 0, t, 1:2])
                    i.then_inc(S["xn_done"], 1)
                if b6 is not None and b6.c % 2 == 1:
                    act.wait_ge(S["gap_done"], pair(b6) + 1)
                    a.activation(exp_gap[:, :], gap[:, :], ACT.Exp).then_inc(S["exp_gap_done"], 1)
                if b4 is not None:
                    h = b4.slot(2)
                    act.wait_ge(S["proj_in_ps"], b4.n + 1)
                    for t in range(TB):
                        i = a.activation(squares[:, h, t, :], proj_ps[h][:, t, 0, :], ACT.Square, scale=D ** -0.5,
                                         accum_out=moments[:, (u + 1) % 2, 1, t, 1:2])
                    i.then_inc(S["moments2_done"], 1)
                if b1 is not None:
                    act.wait_ge(S["xnT_in_ps"], b1.n + 1)
                    a.copy(xnT[:, b1.slot(2), :], xnT_ps).then_inc(S["xnT_done"], 1)
            pass_1(act, step)

            def step(at):
                t3, t5 = at(3), at(5)
                if t5 is not None:
                    h = t5.slot(2)
                    act.wait_ge(S["hid_in_ps"], t5.n + 1)
                    a.activation(hid[:, h, :, :], hid_ps[h], ACT.Gelu).then_inc(S["hid_done"], 1)
                if t3 is not None:
                    h = t3.slot(2)
                    act.wait_ge(S["got_in_ps"], t3.n + 1)
                    a.copy(got_T[:, h, :], got_ps[h]).then_inc(S["got_T_done"], 1)
            pass_2(act, step)

        @block.vector
        def _(dve):
            v = nc.vector
            v.memset(bias3[:, :], 0.0).then_inc(S["bias_step"], 1)
            v.memset(ones_b[:, :], 1.0).then_inc(S["ones_ready"], 1)
            v.memset(ones_h[:, :], 1.0)
            v.memset(v_sb[:, :, :, D:VW], 1.0)
            ROWS = slice(0, 65)

            def split_high(lo, hi, name, at_step):
                v.tensor_copy(bias_h[ROWS, lo:hi], bias_f[ROWS, lo:hi]).then_inc(S[name], 1)
                dve.wait_ge(S[name], at_step + 1)
                v.tensor_tensor(bias_r[ROWS, lo:hi], bias_f[ROWS, lo:hi], bias_h[ROWS, lo:hi], ALU.subtract)\
                 .then_inc(S[name], 1)

            def split_low(lo, hi, name, at_step, ready, by):
                dve.wait_ge(S[name], at_step + 2)
                v.tensor_copy(bias_m[64:65, lo:hi], bias_r[64:65, lo:hi]).then_inc(S[name], 1)
                v.tensor_copy(bias3[0:1, lo:hi], bias_h[0:1, lo:hi])
                dve.wait_ge(S[name], at_step + 3)
                v.tensor_tensor(bias_s[64:65, lo:hi], bias_r[64:65, lo:hi], bias_m[64:65, lo:hi], ALU.subtract)\
                 .then_inc(S[name], 1)
                v.tensor_copy(bias3[32:33, lo:hi], bias_r[32:33, lo:hi])
                dve.wait_ge(S[name], at_step + 4)
                v.tensor_copy(bias3[64:65, lo:hi], bias_s[64:65, lo:hi]).then_inc(S[ready], by)

            def prepare_biases():
                dve.wait_ge(S["bias_in"], 16)
                dve.wait_ge(S["bias_step"], 1)
                v.tensor_scalar_add(bias_f[ROWS, 0:2 * D], bias_f[ROWS, 0:2 * D], 1.0).then_inc(S["bias_step"], 1)
                dve.wait_ge(S["bias_step"], 2)
                split_high(0, 3 * D, "bias_step", 2)

            def finish_biases():
                split_low(0, 3 * D, "bias_step", 2, "dve_const", 2)

            def prepare_projection():
                dve.wait_ge(S["affine_in"], 32)
                dve.wait_ge(S["weights_in"], 48)
                v.tensor_reduce(wproj_mean[:, :], wproj[:, :], AX.X, ALU.add)
                v.tensor_reduce(bias_mean[ROWS, :], bias_f[ROWS, 3 * D:4 * D], AX.X, ALU.add).then_inc(S["proj_step"], 1)
                dve.wait_ge(S["router_mean_in_ps"], 1)
                v.tensor_tensor(wr_c[:, :], wr[:, :], wr_mean_ps, ALU.subtract).then_inc(S["router_const"], 1)

            def finish_projection():
                dve.wait_ge(S["proj_step"], 1)
                v.tensor_scalar_mul(wproj_mean[:, :], wproj_mean[:, :], 1.0 / D)
                v.tensor_scalar_mul(bias_mean[ROWS, :], bias_mean[ROWS, :], 1.0 / D).then_inc(S["proj_step"], 1)
                dve.wait_ge(S["proj_step"], 2)
                v.scalar_tensor_tensor(bias_f[ROWS, 4 * D:5 * D], bias_f[ROWS, 3 * D:4 * D],
                                       bias_mean[ROWS, 0:1], gamma_b[ROWS, :], ALU.subtract, ALU.mult)
                v.tensor_scalar(bias_f[ROWS, 3 * D:4 * D], bias_f[ROWS, 3 * D:4 * D],
                                bias_mean[ROWS, 0:1], None, ALU.subtract).then_inc(S["proj_step"], 1)
                v.tensor_scalar(wproj2[:, 0, :], wproj[:, :], wproj_mean[:, 0:1], None, ALU.subtract)
                v.scalar_tensor_tensor(wproj2[:, 1, :], wproj[:, :], wproj_mean[:, 0:1], gamma_b[:, :],
                                       ALU.subtract, ALU.mult).then_inc(S["proj_const"], 1)

            def split_projection_bias():
                dve.wait_ge(S["proj_step"], 3)
                split_high(3 * D, 5 * D, "proj_step", 3)
                split_low(3 * D, 5 * D, "proj_step", 3, "proj_const", 1)

            def stats(tag, b, out_stat, src):
                for t in range(TB):
                    i = v.bn_stats(out_stat[:, b.slot(2), t, :], src(t))
                i.then_inc(S[f"stats{tag}_done"], 1)

            def aggregate(tag, b, out_mv, stat):
                dve.wait_ge(S[f"stats{tag}_done"], b.n + 1)
                dve.sem_inc(S["passed_gate"], 1)
                for t in range(TB):
                    i = v.bn_aggr(out_mv(t), stat[:, b.slot(2), t, :])
                i.then_inc(S[f"moments{tag}_done"], 1)

            def per_expert(a):
                return a[:, :].unsqueeze(2).to_broadcast([P, PT, E])

            def coefficients(u, b1, b5, b6):
                h = b1.slot(2)
                dve.wait_ge(S["rstd_done"], rounds_of_std(b1, b5, b6))
                v.scalar_tensor_tensor(nb1[:, h, :], moments[:, u % 2, 0, :, 0], -1.0,
                                       moments[:, u % 2, 0, :, 1], ALU.mult, ALU.mult)
                v.tensor_scalar_add(rp1[:, h, :], moments[:, u % 2, 0, :, 1], 1.0).then_inc(S["nb1_done"], 1)

            def step(u, at):
                b0, b1, b2, b3, b4, b5, b6 = at(0), at(1), at(2), at(3), at(4), at(5), at(6)
                closes = b6 is not None and b6.c % 2 == 1
                n = pair(b6) if closes else None
                half = (b6.c // 2) % 2 if closes else None
                if closes:
                    dve.wait_ge(S["logits_in_ps"], b6.n + 1)
                    v.tensor_copy(logits[:, :, :], logit_ps).then_inc(S["logits_read"], 1)
                if closes:
                    dve.wait_ge(S["logits_read"], n + 1)
                    v.tensor_reduce(top1[:, :], logits[:, :, :], AX.X, ALU.max).then_inc(S["top1_done"], 1)
                lo, hi = span(b1, b5, b6)
                if lo < hi:
                    if b1 is not None:
                        dve.wait_ge(S["moments1_done"], b1.n + 1)
                    if b5 is not None:
                        dve.wait_ge(S["moments2_done"], b5.n + 1)
                    if b6 is not None:
                        dve.wait_ge(S["moments3_done"], b6.n + 1)
                    w = moments[:, u % 2, lo:hi, :, 1]
                    v.tensor_scalar_add(w, w, LN_EPS).then_inc(S["eps_added"], 1)
                if b1 is not None and b1.least == 0:
                    prepare_biases()
                if b4 is not None:
                    h = b4.slot(2)
                    dve.wait_ge(S["rden_done"], b4.n + 1)
                    v.tensor_tensor(attn[:, h, :, :].rearrange("p d (t g) -> p t g d", t=TB),
                                    num_ps[:, :, 0:D].rearrange("p t (g d) -> p t g d", g=HEADS),
                                    rden[:, h, :, :].unsqueeze(3).to_broadcast([P, TB, HEADS, HD]),
                                    ALU.mult).then_inc(S["attn_done"], 1)
                if closes:
                    dve.wait_ge(S["top1_done"], n + 1)
                    v.tensor_tensor(is_top[:, :, :], logits[:, :, :], per_expert(top1), ALU.is_equal)\
                     .then_inc(S["is_top_done"], 1)
                if b4 is not None:
                    h = b4.slot(2)
                    dve.wait_ge(S["attn_done"], b4.n + 1)
                    v.transpose(regrouped[:, h, :, :, :].rearrange("p a d r -> p d a r"),
                                attn[:, h, :, :]).then_inc(S["regrouped_done"], 1)
                if closes:
                    if b6.least == 1:
                        dve.wait_ge(S["pool_const"], 5)
                    dve.wait_ge(S["is_top_done"], n + 1)
                    v.tensor_tensor(key[:, :, :], is_top[:, :, :], first_key[:, :, :], ALU.mult)\
                     .then_inc(S["key_done"], 1)
                if b3 is not None:
                    h = b3.slot(2)
                    if b3.least == 0:
                        dve.wait_ge(S["pool_const"], 4)
                    dve.wait_ge(S["sum_in_ps"], b3.n + 1)
                    v.tensor_tensor(kv_sb[:, h, :], sum_ps, head_mask[:, :], ALU.mult)\
                     .then_inc(S["kvsum_done"], 1)
                if closes:
                    dve.wait_ge(S["key_done"], n + 1)
                    v.tensor_reduce(top_key[:, :], key[:, :, :], AX.X, ALU.max).then_inc(S["top_key_done"], 1)
                if b0 is not None:
                    if isinstance(b0.n, int):
                        for c, (first, _) in enumerate(X_CHUNKS):
                            if b0.n == first:
                                dve.wait_ge(x_in[c], 16)
                    stats(1, b0, stat1, lambda t: x_tile(b0, t))
                if b1 is not None and b5 is None:
                    coefficients(u, b1, b5, b6)
                    if b1.least == 0:
                        finish_biases()
                    if b1.least == 1:
                        prepare_projection()
                    if b1.least == 2:
                        split_projection_bias()
                if closes:
                    dve.wait_ge(S["top_key_done"], n + 1)
                    v.tensor_tensor(chosen[:, :, :], key[:, :, :], per_expert(top_key), ALU.is_equal)\
                     .then_inc(S["chosen_done"], 1)
                if closes:
                    dve.wait_ge(S["chosen_done"], n + 1)
                    v.scalar_tensor_tensor(rest[:, :, :], chosen[:, :, :], NEG_HUGE, logits[:, :, :],
                                           ALU.mult, ALU.add).then_inc(S["rest_done"], 1)
                if b5 is not None:
                    dve.wait_ge(S["rstd_done"], rounds_of_std(b1, b5, b6))
                    dve.wait_ge(S["resid_done"], b5.n + 1)
                    dve.wait_ge(rows_free[b5.slot(UB)], 16 * (1 + TB * b5.round()))
                    for t in range(TB):
                        i = v.scalar_tensor_tensor(rows[:, b5.slot(UB), t, 0:D], proj_ps[b5.slot(2)][:, t, 1, :],
                                                   moments[:, u % 2, 1, t, 1:2], resid[:, b5.slot(UB), t, :],
                                                   ALU.mult, ALU.add)
                    i.then_inc(S["x1_done"], 1)
                if b3 is not None:
                    h = b3.slot(2)
                    dve.wait_ge(S["num_in_ps"], b3.n + 1)
                    v.tensor_scalar_max(den[:, h, :, :], num_ps[:, :, D:VW], DEN_MIN).then_inc(S["den_done"], 1)
                if closes:
                    dve.wait_ge(S["rest_done"], n + 1)
                    v.tensor_reduce(top2[:, :], rest[:, :, :], AX.X, ALU.max).then_inc(S["top2_done"], 1)
                if closes:
                    v.tensor_reduce(n_chosen[:, :], chosen[:, :, :].rearrange("p t e -> p e t"), AX.X, ALU.add)\
                     .then_inc(S["n_chosen_done"], 1)
                if closes:
                    dve.wait_ge(S["top2_done"], n + 1)
                    v.tensor_tensor(diff[:, :], top2[:, :], top1[:, :], ALU.subtract).then_inc(S["diff_done"], 1)
                if b0 is not None:
                    if b0.least >= 2:
                        dve.wait_ge(S["xn_done"], b0.n - 1)
                    aggregate(1, b0, lambda t: moments[:, (u + 1) % 2, 0, t, :], stat1)
                if b1 is not None and b5 is not None:
                    coefficients(u, b1, b5, b6)
                if b5 is not None:
                    dve.wait_ge(S["x1_done"], b5.n + 1)
                    stats(3, b5, stat3, lambda t: rows[:, b5.slot(UB), t, 0:D])
                if closes:
                    dve.wait_ge(S["ranks_in_ps"], n + 1)
                    v.tensor_tensor(pos_sel[:, :, :], rank_ps, chosen[:, :, :], ALU.mult)\
                     .then_inc(S["pos_sel_done"], 1)
                if closes:
                    dve.wait_ge(S["row_tail_done"], b6.n + 1)
                    dve.wait_ge(S["diff_done"], n + 1)
                    v.tensor_tensor(gap[:, :].rearrange("p (b t) -> p b t", b=2),
                                    diff[:, :].rearrange("p (b t) -> p b t", b=2),
                                    rows[:, 2 * half:2 * half + 2, :, RSTD], ALU.mult).then_inc(S["gap_done"], 1)
                if b2 is not None:
                    h = b2.slot(2)
                    dve.wait_ge(S["expk_done"], b2.n + 1)
                    v.scalar_tensor_tensor(phi_k[:, h, :, :], exp_k[:, h, :, :], 1.0, kv_ps[:, :, 0:D],
                                           ALU.min, ALU.max).then_inc(S["phik_done"], 1)
                if b3 is not None:
                    h = b3.slot(2)
                    dve.wait_ge(S["den_done"], b3.n + 1)
                    v.reciprocal(rden[:, h, :, :], den[:, h, :, :]).then_inc(S["rden_done"], 1)
                if closes:
                    dve.wait_ge(S["n_chosen_done"], n + 1)
                    v.tensor_tensor(seen[:, :], seen[:, :], n_chosen[:, :], ALU.add).then_inc(S["seen_done"], 1)
                if closes:
                    dve.wait_ge(S["pos_sel_done"], n + 1)
                    with nc.allow_low_precision("row numbers are whole and below 2^24"):
                        v.tensor_reduce(pos[:, half, :], pos_sel[:, :, :], AX.X, ALU.add)
                if closes:
                    dve.wait_ge(S["exp_gap_done"], n + 1)
                    v.tensor_scalar_add(gate_den[:, :], exp_gap[:, :], 1.0).then_inc(S["gate_den_done"], 1)
                if b2 is not None:
                    h = b2.slot(2)
                    dve.wait_ge(S["expq_done"], b2.n + 1)
                    v.scalar_tensor_tensor(phi_q[:, h, :].rearrange("p (c r) -> p r c", r=R),
                                           exp_q[:, h, :].rearrange("p (r c) -> p r c", r=R), 1.0,
                                           q_ps.rearrange("p (r c) -> p r c", r=R), ALU.min, ALU.max)\
                     .then_inc(S["phiq_done"], 1)
                if b2 is not None and b2.least == 0:
                    finish_projection()
                if closes:
                    dve.wait_ge(S["gate_den_done"], n + 1)
                    v.reciprocal(rows[:, 2 * half:2 * half + 2, :, GATE],
                                 gate_den[:, :].rearrange("p (b t) -> p b t", b=2)).then_inc(S["pos_done"], 1)
                if b5 is not None:
                    aggregate(3, b5, lambda t: moments[:, (u + 1) % 2, 2, t, :], stat3)

            pass_1(dve, step)

            count = [0]

            def link(ins):
                count[0] += 1
                ins.then_inc(S["table_step"], 1)
                dve.wait_ge(S["table_step"], count[0])
            v.memset(reached[:, :, 0:1], 1.0)
            dve.wait_ge(S["counts_in_ps"], 1)
            link(v.tensor_tensor(n_tok[:, :], count_ps, region_base[:, :], ALU.subtract))
            link(v.tensor_tensor(over[:, :, :], n_tok[:, :].unsqueeze(2).to_broadcast([P, E, TOK // P]),
                                 step_128[:, :, :], ALU.is_gt))
            link(v.tensor_reduce(n_tiles[:, :], over[:, :, :], AX.X, ALU.add))
            link(v.tensor_tensor(tiles_m[:, :, :], n_tiles[:, :].unsqueeze(1).to_broadcast([P, E, E]),
                                 upto[:, :, :], ALU.mult))
            link(v.tensor_reduce(tiles_upto[:, :], tiles_m[:, :, :], AX.X, ALU.add))
            v.tensor_tensor(reached[:, :, 1:E + 1], tile_no[:, :].unsqueeze(2).to_broadcast([P, NT, E]),
                            tiles_upto[:, :].unsqueeze(1).to_broadcast([P, NT, E]), ALU.is_ge)
            link(v.tensor_tensor(tiles_before[:, :], tiles_upto[:, :], n_tiles[:, :], ALU.subtract))
            v.tensor_tensor(mine[:, :, :], reached[:, :, 0:E], reached[:, :, 1:E + 1], ALU.subtract)
            link(v.scalar_tensor_tensor(row_base[:, :], tiles_before[:, :], float(P), count_ps, ALU.mult, ALU.add))
            link(v.tensor_tensor(row_of[:, :, :], row_base[:, :].unsqueeze(1).to_broadcast([P, NT, E]),
                                 tile_end[:, :].unsqueeze(2).to_broadcast([P, NT, E]), ALU.subtract))
            v.tensor_reduce(passed[:, :], reached[:, :, 1:E + 1], AX.X, ALU.add)
            link(v.tensor_tensor(row_sel[:, :, :], row_of[:, :, :], mine[:, :, :], ALU.mult))
            v.tensor_scalar_min(tile_expert[:, :], passed[:, :], float(E - 1))
            with nc.allow_low_precision("row numbers are whole and below 2^24"):
                v.tensor_reduce(tile_row[:, :], row_sel[:, :, :], AX.X, ALU.add).then_inc(S["table_done"], 1)
            dve.wait_ge(S["table_done"], 1)
            dve.wait_ge(S["ffn_in"], 32)

            def load_w1(t):
                expert = dve.value_load(tile_expert[0:1, bass.ds(t.n, 1)], min_val=0, max_val=E - 1)
                if t.least >= 2:
                    dve.wait_ge(S["hid_in_ps"], t.n - 1)
                v.tensor_copy(w1_tile[:, t.slot(2), :], w1_sb[:, bass.ds(expert * HID, HID)])\
                 .then_inc(S["w1_tile_done"], 1)
            load_w1(Item(UT, 0, 0))
            load_w1(Item(UT, 0, 1))

            def step(at):
                t2, t3, t5 = at(2), at(3), at(5)
                if t3 is not None and t3.least >= 2:
                    load_w1(t3)
                if t2 is not None:
                    h = t2.slot(2)
                    s = t2.slot(UT)
                    dve.wait_ge(got_in[s], 16 * (t2.round() + 1))
                    if t2.least >= 2:
                        dve.wait_ge(S["got_in_ps"], t2.n - 1)
                    v.tensor_scalar(got_n[:, h, :], got[:, s, 0:D], got[:, s, MEAN:MEAN + 1],
                                    got[:, s, RSTD:RSTD + 1], ALU.subtract, ALU.mult).then_inc(S["got_n_done"], 1)
                if t5 is not None:
                    h = t5.slot(2)
                    s = t5.slot(UT)
                    dve.wait_ge(S["y_in_ps"], t5.n + 1)
                    if t5.least >= UT:
                        dve.wait_ge(out_done[s], 16 * t5.round())
                    v.tensor_copy(done_token[:, s:s + 1], got[:, s, TOKEN:TOKEN + 1].bitcast(I32))
                    v.scalar_tensor_tensor(done[:, s, :], y_ps[h], got[:, s, GATE:GATE + 1], got[:, s, 0:D],
                                           ALU.mult, ALU.add).then_inc(S["done_ready"], 1)
            pass_2(dve, step)


def kernel(L0_attn_H, L0_attn_W_qkv, L0_attn_b_qkv, L0_attn_W_proj, L0_attn_b_proj, L0_attn_gamma,
           L0_attn_beta, L0_ffn_Wr, L0_ffn_W1, L0_ffn_W2):
    import numpy as np
    import concourse.bacc as bacc
    from concourse.bass_utils import run_bass_kernel_spmd as run

    H = np.asarray(L0_attn_H)
    B, N, D = H.shape
    W1, W2 = np.asarray(L0_ffn_W1), np.asarray(L0_ffn_W2)
    E, _, HID = W1.shape
    bias = np.concatenate([np.asarray(L0_attn_b_qkv), np.asarray(L0_attn_b_proj)])
    split = (B, 16, 2, 4, 2, D)
    x = H.reshape(split).transpose(3, 2, 1, 0, 4, 5).reshape(128, B, 2 * D)
    wproj_t = np.asarray(L0_attn_W_proj).T.reshape(2, 4, 2, 8, D).transpose(3, 2, 1, 0, 4).reshape(D, D)
    arrays = {
        "x": x,
        "wqkv_t": np.asarray(L0_attn_W_qkv).T,
        "b_all": bias,
        "wproj_t": wproj_t,
        "gamma": np.asarray(L0_attn_gamma),
        "beta": np.asarray(L0_attn_beta),
        "w_router": np.asarray(L0_ffn_Wr),
        "w1": W1.transpose(1, 0, 2).reshape(D, E * HID),
        "w2": W2.reshape(E, HID // 128, 128, D).transpose(2, 0, 1, 3).reshape(128, E * HID),
    }
    arrays = {k: np.ascontiguousarray(a) for k, a in arrays.items()}
    nc = bacc.Bacc("TRN2", target_bir_lowering=False, num_devices=1)
    args = [nc.dram_tensor(k, a.shape, F32, kind="ExternalInput").ap() for k, a in arrays.items()]
    args.append(nc.dram_tensor("out", [B * N, D], F32, kind="ExternalOutput").ap())
    build(nc, *args)
    r = run(nc, [arrays], core_ids=[0])
    return r.results[0]["out"].reshape(B, 4, 2, 16, 2, D).transpose(0, 3, 2, 1, 4, 5).reshape(H.shape)
```
